# Optimizing a Trainium2 kernel written in Bass

```python
import numpy as np
import jax
import jax.numpy as jnp

def _softmax(x, axis=-1):
    return jax.nn.softmax(x, axis=axis)

def _gelu(x):
    return jax.nn.gelu(x, approximate=True)

def _silu(x):
    return jax.nn.silu(x)

def _sigmoid(x):
    return jax.nn.sigmoid(x)

def _layernorm(x, axis=-1, eps=1e-05):
    m = jnp.mean(x, axis=axis, keepdims=True)
    v = jnp.var(x, axis=axis, keepdims=True)
    return (x - m) / jnp.sqrt(v + eps)

def _scatter_add(tgt, idx, src, axis=0):
    return tgt.at[idx].add(src)

def _segment_sum(src, seg, n):
    return jax.ops.segment_sum(src, seg, n)
kernel_name = 'mk_conv_preact_d1_conv_nchw768_r2_e411df'

def setup_inputs(seed: int=0):
    np.random.seed(seed)
    _w = jnp.asarray

    def _rec_inputs():
        import jax
        import jax.numpy as jnp
        _gk = jax.random.key(seed)
        x = -0.0002221 + 1 * jax.random.normal(jax.random.fold_in(_gk, 1), (32, 384, 32, 32), jnp.float32)
        return x
    x = _rec_inputs()

    def _L0_conv_setup():
        import jax, jax.numpy as jnp
        import numpy as np
        DIM = 384
        HEADS = 12
        B, C, H, W = (32, DIM, 32, 32)
        key = jax.random.key(seed)
        k1, k2, k3, k4 = jax.random.split(key, 4)
        x = jax.random.normal(k1, (B, C, H, W), dtype=jnp.float32)
        scale = 1.0 / np.sqrt(DIM)
        qkv_w = jax.random.normal(k2, (DIM, DIM), dtype=jnp.float32) * scale
        temp = jnp.ones((HEADS, 1), dtype=jnp.float32)
        out_w = jax.random.normal(k3, (DIM, DIM), dtype=jnp.float32) * scale
        out_b = jax.random.normal(k4, (DIM,), dtype=jnp.float32) * 0.01
        return {'x': x, 'qkv_w': qkv_w, 'temp': temp, 'out_w': out_w, 'out_b': out_b}
    _L0_conv_all = _L0_conv_setup()
    _L0_conv_in = {k: v for k, v in _L0_conv_all.items() if k in ('qkv_w', 'temp', 'out_w', 'out_b')}
    del _L0_conv_all
    return {'x': x, 'L0_conv_qkv_w': _L0_conv_in['qkv_w'], 'L0_conv_temp': _L0_conv_in['temp'], 'L0_conv_out_w': _L0_conv_in['out_w'], 'L0_conv_out_b': _L0_conv_in['out_b']}

def reference(x, L0_conv_qkv_w, L0_conv_temp, L0_conv_out_w, L0_conv_out_b):
    import jax
    import jax.numpy as jnp

    def _L0_conv_ref(x, qkv_w, temp, out_w, out_b):
        import jax, jax.numpy as jnp
        import numpy as np
        DIM = 384
        HEADS = 12
        B, C, H, W = (32, DIM, 32, 32)
        b, c, hh, ww = x.shape
        n = hh * ww
        d = c // HEADS
        xt = x.reshape(b, c, n).transpose(0, 2, 1)
        w = jnp.einsum('bnc,oc->bno', xt, qkv_w).reshape(b, n, HEADS, d).transpose(0, 2, 1, 3)
        norm = jnp.sqrt(jnp.sum(w * w, axis=-2, keepdims=True))
        w_normed = w / jnp.maximum(norm, 1e-12)
        s = jnp.sum(w_normed * w_normed, axis=-1)
        Pi = jax.nn.softmax(s * temp[None, :, :], axis=1)
        Pi_n = Pi / (jnp.sum(Pi, axis=-1, keepdims=True) + 1e-08)
        dots = jnp.einsum('bhn,bhnd->bhd', Pi_n, w * w)[:, :, None, :]
        attn = 1.0 / (1.0 + dots)
        out = -(w * Pi[..., None]) * attn
        out = out.transpose(0, 2, 1, 3).reshape(b, n, c)
        out = jnp.einsum('bnc,oc->bno', out, out_w) + out_b
        return out.transpose(0, 2, 1).reshape(b, c, hh, ww)

    def _gn(v, G=32, eps=1e-05):
        B_, C_, H_, W_ = v.shape
        g = v.reshape(B_, G, C_ // G, H_, W_)
        m = jnp.mean(g, axis=(2, 3, 4), keepdims=True)
        s = jnp.var(g, axis=(2, 3, 4), keepdims=True)
        return ((g - m) / jnp.sqrt(s + eps)).reshape(v.shape)

    def _ln_c(v, eps=1e-06):
        m = jnp.mean(v, axis=1, keepdims=True)
        s = jnp.var(v, axis=1, keepdims=True)
        return (v - m) / jnp.sqrt(s + eps)

    def _ln_t(v, eps=1e-05):
        m = jnp.mean(v, axis=-1, keepdims=True)
        s = jnp.var(v, axis=-1, keepdims=True)
        return (v - m) / jnp.sqrt(s + eps)

    def _to_tokens(v):
        B_, C_, H_, W_ = v.shape
        return v.reshape(B_, C_, H_ * W_).transpose(0, 2, 1)

    def _from_tokens(t, like):
        B_, C_, H_, W_ = like.shape
        return t.transpose(0, 2, 1).reshape(B_, C_, H_, W_)
    x = x + _L0_conv_ref(_gn(x), L0_conv_qkv_w, L0_conv_temp, L0_conv_out_w, L0_conv_out_b)
    return x

_drawn_inputs = setup_inputs


def setup_inputs(seed=0):
    import zlib

    import numpy as np

    out = dict(_drawn_inputs(seed))
    spreads = {'L0_conv_temp': (1.0, 0.6)}
    factors = {'L0_conv_out_b': 6.263}
    for name, (base, spread) in spreads.items():
        noise = np.random.default_rng([zlib.crc32(name.encode()), seed]).standard_normal(out[name].shape)
        drawn = base * np.exp(spread * noise) if base else spread * noise
        out[name] = jnp.asarray(drawn.astype(out[name].dtype))
    for name, factor in factors.items():
        out[name] = (out[name] * factor).astype(out[name].dtype)
    return out
```

```python
from contextlib import ExitStack

import concourse.bass as bass
from concourse import mybir

ALU = mybir.AluOpType
ACT = mybir.ActivationFunctionType
F32 = mybir.dt.float32
F32R = mybir.dt.float32r
I32 = mybir.dt.int32
AX_X = mybir.AxisListType.X

P = 128
GROUPS = 32
GN_EPS = 1e-5
NORM_FLOOR = 1e-12
SUM_FLOOR = 1e-8
SLOTS = 4
BANK = 512
QUAD = 32
RSQRT_SEED = 0x5F3759DF
NEWTON = 3

GN_AGGREGATED, GN_SPREAD, GN_STEPS = 2, 5, 9 + 3 * NEWTON
HEADSUM_STEPS = 4
SM_SHIFTED, SM_PI, SM_PI_SUM, SM_STEPS = 3, 6, 7, 11
U_STEPS = 4


class Image:

    def __init__(self, number, slot):
        self.number, self.slot = number, slot % SLOTS

    def __add__(self, n):
        return Image(self.number + n, self.slot + n)

    def __sub__(self, n):
        return self + -n

    def counts(self, each, more=0):
        return self.number * each + more

    def of(self, dram):
        known = isinstance(self.number, int)
        return dram[self.number] if known else dram[bass.ds(self.number, 1)].squeeze(0)


def conv_attention(nc, x, qkv_w, temp, out_w, out_b, y):
    B, C, H, W = x.shape
    N = H * W
    HEADS = temp.shape[0]
    D = C // HEADS
    T = C // P
    HPT = P // D
    HALVES = N // BANK
    BLOCKS = N // P
    QUADS = P // QUAD
    PER_GROUP = C // GROUPS // T
    assert D == QUAD and T * P == C and HALVES * BANK == N and PER_GROUP * GROUPS == P

    x_img = x.rearrange("b (p t) h w -> b p (t h w)", t=T)
    y_img = y.rearrange("b (p t) h w -> b p (t h w)", t=T)

    with ExitStack() as ctx:
        def sb(name, shape, dt=F32):
            return ctx.enter_context(nc.sbuf_tensor(name, shape, dt))

        def pb(name, shape):
            return ctx.enter_context(nc.psum_tensor(name, shape, F32))

        def sem(name):
            return ctx.enter_context(nc.semaphore(name))

        X = sb("X", [P, SLOTS, T * N])
        XN = sb("XN", [P, T, N])
        XH = sb("XH", [P, T, N], F32R)
        XL = sb("XL", [P, T, N], F32R)
        WV = sb("WV", [P, T, N])
        WS = sb("WS", [P, T, N])
        U = sb("U", [P, T, N])
        UH = sb("UH", [P, T, N], F32R)
        UL = sb("UL", [P, T, N], F32R)
        W1H = sb("W1H", [P, T, C], F32R)
        W1L = sb("W1L", [P, T, C], F32R)
        W2H = sb("W2H", [P, T, C], F32R)
        W2L = sb("W2L", [P, T, C], F32R)
        identity = sb("identity", [P, P])
        group_mean = sb("group_mean", [P, P])
        head_mask = sb("head_mask", [P, T, QUAD])
        ones = sb("ones", [P, P])
        temp_row = sb("temp_row", [1, HEADS])
        temp_o = sb("temp_o", [P, T])
        bias = sb("bias", [P, T])
        stats = sb("stats", [P, T * HALVES, 6])
        part_mv = sb("part_mv", [P, 2])
        wait_cell = sb("wait_cell", [P, 1])
        gmean = sb("gmean", [P, 1])
        dmean = sb("dmean", [P, 1])
        spread = sb("spread", [P, 1])
        gvar = sb("gvar", [P, 1])
        seed = sb("seed", [P, 1])
        root = sb("root", [P, 1])
        root_t = sb("root_t", [P, 2])
        rstd = sb("rstd", [P, 1])
        shift = sb("shift", [P, 1])
        sumsq = sb("sumsq", [P, T])
        inv = sb("inv", [P, 3, T])
        headsum = sb("headsum", [P, T, QUAD])
        ST = sb("ST", [P, BLOCKS, QUAD])
        smax = sb("smax", [P, BLOCKS])
        SE = sb("SE", [P, BLOCKS, HEADS])
        EX = sb("EX", [P, BLOCKS, HEADS])
        ssum = sb("ssum", [P, BLOCKS])
        srec = sb("srec", [P, BLOCKS])
        PI = sb("PI", [P, BLOCKS, HEADS])
        pi_sum = sb("pi_sum", [P, HEADS])
        PIX = sb("PIX", [P, T, BLOCKS, P])
        pick = sb("pick", [P, T, HEADS])
        pi_tot = sb("pi_tot", [P, 3, T])
        dots = sb("dots", [P, 3, T])

        acc = pb("acc", [P, 2, N])
        pi_b = pb("pi_b", [P, N])
        scores = pb("scores", [P, BANK])
        small = pb("small", [P, BANK])
        gn_ps = small[:, 0:2]
        tot_ps = small[:, 16:16 + HEADS]
        temp_ps = small[:, 32:32 + HEADS]

        x_loaded = sem("x_loaded")
        y_stored = sem("y_stored")
        w1_loaded = sem("w1_loaded")
        w2_loaded = sem("w2_loaded")
        consts_loaded = sem("consts_loaded")
        masks_step = sem("masks_step")
        ones_set = sem("ones_set")
        temp_spread = sem("temp_spread")
        temp_kept = sem("temp_kept")
        weights_turned = sem("weights_turned")
        weights_hi = sem("weights_hi")
        weights_lo = sem("weights_lo")
        gn_step = sem("gn_step")
        gmean_done = sem("gmean_done")
        gvar_done = sem("gvar_done")
        xn_done = sem("xn_done")
        xh_done = sem("xh_done")
        xl_done = sem("xl_done")
        m1_done = sem("m1_done")
        squared = sem("squared")
        w_kept = sem("w_kept")
        headsum_step = sem("headsum_step")
        scores_done = sem("scores_done")
        sm_step = sem("sm_step")
        exp_done = sem("exp_done")
        pi_widened = sem("pi_widened")
        tot_done = sem("tot_done")
        pi_spread = sem("pi_spread")
        u_step = sem("u_step")
        uh_done = sem("uh_done")
        ul_done = sem("ul_done")
        m2_done = sem("m2_done")
        y_done = sem("y_done")

        def turned(k):
            return acc[:, k // 2, (k % 2) * BANK:(k % 2) * BANK + C] if k < 4 else \
                pi_b[:, (k - 4) * BANK:(k - 4) * BANK + C]

        def wait(eng, semaphore, value):
            if not isinstance(value, int) or value > 0:
                eng.wait_ge(semaphore, value)

        def has(j):
            return not isinstance(j.number, int) or 0 <= j.number < B

        def x_tile(j, t):
            return X[:, j.slot, t * N:(t + 1) * N]

        def pipeline(eng, step, first, last):
            loop_first, loop_end = 2, B - 2
            assert (loop_end - loop_first) % SLOTS == 0
            for i in range(first, loop_first):
                step(Image(i, i))
            with eng.Fori(loop_first, loop_end - SLOTS + 1, SLOTS) as i:
                for k in range(SLOTS):
                    step(Image(i + k, loop_first + k))
            for i in range(loop_end, last + 1):
                step(Image(i, i))

        block = ctx.enter_context(nc.Block())

        @block.sync
        def _(sp):
            sp.dma_start(WV[:].rearrange("p t n -> p (t n)")[:, 0:T * C].rearrange("p (t c) -> p t c", t=T),
                         qkv_w.rearrange("(t p) c -> p t c", t=T)).then_inc(w1_loaded, 16)
            sp.dma_start(WS[:].rearrange("p t n -> p (t n)")[:, 0:T * C],
                         out_w.rearrange("(p t) o -> p (t o)", t=T)).then_inc(w2_loaded, 16)

            def load(j):
                if has(j):
                    wait(sp, x_loaded, j.counts(16))
                    sp.dma_start(X[:, j.slot, :], j.of(x_img)).then_inc(x_loaded, 16)

            def step(i):
                j = i - 2
                if has(j):
                    wait(sp, y_done, j.counts(T, T))
                    sp.dma_start(j.of(y_img), X[:, j.slot, :]).then_inc(y_stored, 16)
                    wait(sp, y_stored, j.counts(16, 16))
                load(i + 2)

            for j in range(3):
                load(Image(j, j))
            pipeline(sp, step, 1, B + 1)

        @block.gpsimd
        def _(pool):
            pool.memset(identity[:], 0.0).then_inc(masks_step, 1)
            pool.memset(group_mean[:], 1.0 / PER_GROUP).then_inc(masks_step, 1)
            pool.memset(head_mask[:], 1.0).then_inc(masks_step, 1)
            pool.wait_ge(masks_step, 3)
            groups = group_mean[:].rearrange("p (g k) -> p g k", k=PER_GROUP)
            pool.affine_select(out=identity[:], in_=identity[:], compare_op=ALU.not_equal, fill=1.0, base=0,
                               pattern=[[-1, P]], channel_multiplier=1).then_inc(masks_step, 1)
            pool.affine_select(out=groups, in_=groups, compare_op=ALU.is_ge, fill=0.0, base=0,
                               pattern=[[-PER_GROUP, GROUPS], [0, PER_GROUP]],
                               channel_multiplier=1).then_inc(masks_step, 1)
            pool.affine_select(out=head_mask[:], in_=head_mask[:], compare_op=ALU.is_ge, fill=0.0, base=0,
                               pattern=[[P, T], [-D, QUAD]], channel_multiplier=1).then_inc(masks_step, 1)
            pool.wait_ge(masks_step, 6)
            pool.affine_select(out=groups, in_=groups, compare_op=ALU.is_ge, fill=0.0, base=PER_GROUP - 1,
                               pattern=[[PER_GROUP, GROUPS], [0, PER_GROUP]],
                               channel_multiplier=-1).then_inc(masks_step, 1)
            pool.affine_select(out=head_mask[:], in_=head_mask[:], compare_op=ALU.is_ge, fill=0.0, base=D - 1,
                               pattern=[[-P, T], [D, QUAD]], channel_multiplier=-1).then_inc(masks_step, 1)

            def step(i):
                j = i - 1
                if has(j):
                    for t in range(T):
                        wait(pool, u_step, U_STEPS * j.counts(T, t + 1))
                        wait(pool, uh_done, j.counts(T, t + 1))
                        wait(pool, m2_done, j.counts(T))
                        pool.tensor_tensor(UL[:, t, :], U[:, t, :], UH[:, t, :].bitcast(F32),
                                           ALU.subtract).then_inc(ul_done, 1)
                j = i + 1
                if has(j):
                    for t in range(T):
                        wait(pool, xn_done, j.counts(T, t + 1))
                        wait(pool, xh_done, j.counts(T, t + 1))
                        wait(pool, m1_done, j.counts(T))
                        pool.tensor_tensor(XL[:, t, :], XN[:, t, :], XH[:, t, :].bitcast(F32),
                                           ALU.subtract).then_inc(xl_done, 1)

            pipeline(pool, step, -1, B)

        @block.scalar
        def _(act):
            act.dma_start(temp_row[:], temp.rearrange("h a -> a h")).then_inc(consts_loaded, 16)
            act.dma_start(bias[:], out_b.rearrange("(p t) -> p t", t=T)).then_inc(consts_loaded, 16)
            for k in range(2 * T):
                act.wait_ge(weights_turned, k + 1)
                act.activation(W1H[:, k, :] if k < T else W2H[:, k - T, :], turned(k), ACT.Copy,
                               scale=1.0 if k < T else -1.0).then_inc(weights_hi, 1)

            def step(i):
                def u_hi(t):
                    j = i - 1
                    if has(j):
                        wait(act, u_step, U_STEPS * j.counts(T, t + 1))
                        wait(act, m2_done, j.counts(T))
                        wait(act, ul_done, j.counts(T, t + 1 - T))
                        act.activation(UH[:, t, :], U[:, t, :], ACT.Copy).then_inc(uh_done, 1)

                def keep_w(t):
                    if has(i):
                        wait(act, m1_done, i.counts(T, t + 1))
                        wait(act, u_step, U_STEPS * i.counts(T, t + 1 - T))
                        wait(act, scores_done, i.counts(1))
                        wait(act, headsum_step, i.counts(HEADSUM_STEPS))
                        act.activation(WS[:, t, :], acc[:, t % 2, :], ACT.Square,
                                       accum_out=sumsq[:, t:t + 1]).then_inc(squared, 1)
                        act.activation(WV[:, t, :], acc[:, t % 2, :], ACT.Copy).then_inc(w_kept, 1)

                def normalise(t):
                    j = i + 1
                    if has(j):
                        wait(act, gn_step, j.counts(GN_STEPS, GN_STEPS))
                        wait(act, xl_done, j.counts(T, t + 1 - T))
                        act.activation(XN[:, t, :], x_tile(j, t), ACT.Identity, bias=shift[:, 0:1],
                                       scale=rstd[:, 0:1]).then_inc(xn_done, 1)
                        wait(act, m1_done, j.counts(T))
                        act.activation(XH[:, t, :], x_tile(j, t), ACT.Identity, bias=shift[:, 0:1],
                                       scale=rstd[:, 0:1]).then_inc(xh_done, 1)

                def widen_pi(t):
                    if has(i):
                        wait(act, sm_step, i.counts(SM_STEPS, SM_PI))
                        wait(act, pi_spread, i.counts(T, t + 1 - T))
                        act.activation(PIX[:, t, :, :].rearrange("p b (h d) -> p b h d", d=D),
                                       PI[:, :, t * HPT:(t + 1) * HPT].unsqueeze(3).to_broadcast([P, BLOCKS, HPT, D]),
                                       ACT.Copy).then_inc(pi_widened, 1)

                u_hi(0)
                keep_w(0)
                u_hi(1)
                keep_w(1)
                u_hi(2)
                keep_w(2)
                normalise(0)
                if has(i):
                    wait(act, sm_step, i.counts(SM_STEPS, SM_SHIFTED))
                    act.activation(EX[:], SE[:], ACT.Exp).then_inc(exp_done, 1)
                normalise(1)
                widen_pi(0)
                normalise(2)
                widen_pi(1)
                widen_pi(2)

            pipeline(act, step, -1, B)

        @block.tensor
        def _(pe):
            raw1 = WV[:].rearrange("p t n -> p (t n)")[:, 0:T * C].rearrange("p (o c k) -> p k o c", o=T, k=T)
            raw2 = WS[:].rearrange("p t n -> p (t n)")[:, 0:T * C].rearrange("p (m o c) -> p o m c", m=T, o=T)
            pe.wait_ge(masks_step, 8)
            pe.wait_ge(w1_loaded, 16)
            for k in range(2 * T):
                if k == T:
                    pe.wait_ge(w2_loaded, 16)
                for m in range(T):
                    raw = raw1[:, k, m, :] if k < T else raw2[:, k - T, m, :]
                    last = pe.transpose(turned(k)[:, m * P:(m + 1) * P], raw, identity[:])
                last.then_inc(weights_turned, 1)
            pe.wait_ge(consts_loaded, 32)
            pe.wait_ge(ones_set, 1)
            pe.matmul(temp_ps, ones[0:1, :], temp_row[0:1, :], start=True, stop=True).then_inc(temp_spread, 1)

            def product(out, m, left, right):
                terms = [(left[0], right[0]), (left[1], right[0]), (left[0], right[1])]
                for n, (w, r) in enumerate(terms):
                    for k in range(T):
                        for h in range(HALVES):
                            last = pe.matmul(out[:, h * BANK:(h + 1) * BANK], w[:, k, m * P:(m + 1) * P],
                                             r[:, k, h * BANK:(h + 1) * BANK], start=(n == 0 and k == 0),
                                             stop=(n == 2 and k == T - 1))
                return last

            def step(i):
                before = i - 1

                def first_product(t):
                    if has(i):
                        wait(pe, xh_done, i.counts(T, T))
                        wait(pe, xl_done, i.counts(T, T))
                        if t < 2:
                            wait(pe, y_done, i.counts(T, t + 2 - 2 * T))
                        else:
                            wait(pe, squared, i.counts(T, t - 1))
                            wait(pe, w_kept, i.counts(T, t - 1))
                        product(acc[:, t % 2, :], t, (W1H, W1L), (XH, XL)).then_inc(m1_done, 1)

                def second_product(t):
                    if has(before):
                        wait(pe, uh_done, before.counts(T, T))
                        wait(pe, ul_done, before.counts(T, T))
                        if t < 2:
                            wait(pe, w_kept, i.counts(T, t + 2) if has(i) else B * T)
                            wait(pe, squared, i.counts(T, t + 2) if has(i) else B * T)
                        if t > 0:
                            wait(pe, y_done, before.counts(T, t - 1))
                        product(acc[:, (t + 1) % 2, :], t, (W2H, W2L), (UH, UL)).then_inc(m2_done, 1)

                def spread_pi(j, t):
                    if has(j):
                        wait(pe, pi_widened, j.counts(T, t + 1))
                        wait(pe, u_step, U_STEPS * j.counts(T, t))
                        for b in range(BLOCKS):
                            last = pe.transpose(pi_b[:, b * P:(b + 1) * P],
                                                PIX[:, t, b, :], identity[:])
                        last.then_inc(pi_spread, 1)

                after = i + 1
                first_product(0)
                spread_pi(before, 2)
                first_product(1)
                first_product(2)
                if has(after):
                    wait(pe, gn_step, after.counts(GN_STEPS, GN_AGGREGATED))
                    pe.matmul(gn_ps[:, 0:1], group_mean[:], part_mv[:, 0:1], start=True, stop=True).then_inc(gmean_done, 1)
                second_product(0)
                if has(after):
                    wait(pe, gn_step, after.counts(GN_STEPS, GN_SPREAD))
                    pe.matmul(gn_ps[:, 1:2], group_mean[:], spread[:], start=True, stop=True).then_inc(gvar_done, 1)
                if has(i):
                    wait(pe, headsum_step, i.counts(HEADSUM_STEPS, HEADSUM_STEPS))
                    wait(pe, squared, i.counts(T, T))
                    wait(pe, sm_step, i.counts(SM_STEPS, 1 - SM_STEPS))
                    for t in range(T):
                        for q in range(QUADS):
                            block_q = WS[:, t, :].rearrange("p (b q r) -> p q b r", q=QUADS, r=QUAD)[:, q]
                            last = pe.matmul(scores[q * QUAD:(q + 1) * QUAD, 0:N // QUADS], headsum[:, t, :],
                                             block_q, start=(t == 0), stop=(t == T - 1))
                    last.then_inc(scores_done, 1)
                second_product(1)
                if has(i):
                    wait(pe, sm_step, i.counts(SM_STEPS, SM_PI_SUM))
                    pe.matmul(tot_ps, ones[:], pi_sum[:], start=True, stop=True).then_inc(tot_done, 1)
                spread_pi(i, 0)
                second_product(2)
                spread_pi(i, 1)

            pipeline(pe, step, -1, B)

        @block.vector
        def _(dve):
            def at_channels(out, per_head):
                return dve.tensor_tensor(out, head_mask[:, :, 0:HEADS],
                                         per_head.unsqueeze(1).to_broadcast([P, T, HEADS]), ALU.mult)

            dve.memset(ones[:], 1.0).then_inc(ones_set, 1)
            for k in range(2 * T):
                dve.wait_ge(weights_hi, k + 1)
                hi, lo = (W1H[:, k, :], W1L[:, k, :]) if k < T else (W2H[:, k - T, :], W2L[:, k - T, :])
                dve.scalar_tensor_tensor(lo, turned(k), 1.0 if k < T else -1.0, hi.bitcast(F32), ALU.mult,
                                         ALU.subtract).then_inc(weights_lo, 1)
            dve.wait_ge(temp_spread, 1)
            at_channels(pick[:], temp_ps).then_inc(temp_kept, 1)
            dve.wait_ge(temp_kept, 1)
            dve.tensor_reduce(temp_o[:], pick[:], AX_X, ALU.add).then_inc(temp_kept, 1)
            dve.wait_ge(temp_kept, 2)

            def chain(semaphore, base):
                done = [0]

                def link(instruction, follows=True):
                    done[0] += 1
                    instruction.then_inc(semaphore, 1)
                    if follows:
                        dve.wait_ge(semaphore, base + done[0])
                return link

            def group_stats(j):
                if not has(j):
                    return
                link = chain(gn_step, j.counts(GN_STEPS))
                wait(dve, x_loaded, j.counts(16, 16))
                for t in range(T):
                    for h in range(HALVES):
                        last = dve.bn_stats(stats[:, t * HALVES + h, :], x_tile(j, t)[:, h * BANK:(h + 1) * BANK])
                link(last)
                dve.memset(wait_cell[:], 0.0)
                link(dve.bn_aggr(part_mv[:], stats[:].rearrange("p k s -> p (k s)")), follows=False)

            def group_norm(j):
                if not has(j):
                    return
                link = chain(gn_step, j.counts(GN_STEPS, GN_AGGREGATED))
                wait(dve, gmean_done, j.counts(1, 1))
                link(dve.tensor_copy(gmean[:], gn_ps[:, 0:1]))
                link(dve.tensor_tensor(dmean[:], part_mv[:, 0:1], gmean[:], ALU.subtract))
                link(dve.scalar_tensor_tensor(spread[:], dmean[:], dmean[:, 0:1], part_mv[:, 1:2], ALU.mult, ALU.add),
                     follows=False)
                wait(dve, gvar_done, j.counts(1, 1))
                link(dve.tensor_scalar(gvar[:], gn_ps[:, 1:2], GN_EPS, None, ALU.add))
                link(dve.tensor_scalar(seed[:].bitcast(I32), gvar[:].bitcast(I32), 1, None, ALU.logical_shift_right))
                link(dve.tensor_scalar(root[:].bitcast(I32), seed[:].bitcast(I32), -1.0, float(RSQRT_SEED),
                                       ALU.mult, ALU.add))
                for n in range(NEWTON):
                    link(dve.scalar_tensor_tensor(root_t[:, 0:1], root[:], root[:, 0:1], gvar[:], ALU.mult, ALU.mult))
                    link(dve.tensor_scalar(root_t[:, 1:2], root_t[:, 0:1], -0.5, 1.5, ALU.mult, ALU.add))
                    if n == NEWTON - 1:
                        wait(dve, xh_done, j.counts(T))
                    link(dve.tensor_tensor(rstd[:] if n == NEWTON - 1 else root[:], root[:], root_t[:, 1:2], ALU.mult))
                link(dve.scalar_tensor_tensor(shift[:], gmean[:], -1.0, rstd[:], ALU.mult, ALU.mult), follows=False)

            def head_sum_weights(j):
                if not has(j):
                    return
                link = chain(headsum_step, j.counts(HEADSUM_STEPS))
                wait(dve, squared, j.counts(T, T))
                link(dve.tensor_scalar(inv[:, 0, :], sumsq[:], NORM_FLOOR ** 2, None, ALU.max))
                link(dve.reciprocal(inv[:, 1, :], inv[:, 0, :]))
                link(dve.tensor_tensor(inv[:, 2, :], inv[:, 1, :], temp_o[:], ALU.mult))
                wait(dve, scores_done, j.counts(1))
                link(dve.tensor_tensor(headsum[:], head_mask[:],
                                       inv[:, 2, :].unsqueeze(2).to_broadcast([P, T, QUAD]), ALU.mult), follows=False)

            def softmax_shift(j):
                if not has(j):
                    return
                link = chain(sm_step, j.counts(SM_STEPS))
                wait(dve, scores_done, j.counts(1, 1))
                link(dve.transpose(ST[:].rearrange("p b h -> p (b h)"), scores[:, 0:N // QUADS]))
                link(dve.tensor_reduce(smax[:], ST[:, :, 0:HEADS], AX_X, ALU.max))
                link(dve.tensor_tensor(SE[:], ST[:, :, 0:HEADS],
                                       smax[:].unsqueeze(2).to_broadcast([P, BLOCKS, HEADS]), ALU.subtract),
                     follows=False)

            def softmax_divide(j):
                if not has(j):
                    return
                link = chain(sm_step, j.counts(SM_STEPS, SM_SHIFTED))
                wait(dve, exp_done, j.counts(1, 1))
                link(dve.tensor_reduce(ssum[:], EX[:], AX_X, ALU.add))
                link(dve.reciprocal(srec[:], ssum[:]))
                wait(dve, pi_widened, j.counts(T))
                link(dve.tensor_tensor(PI[:], EX[:], srec[:].unsqueeze(2).to_broadcast([P, BLOCKS, HEADS]), ALU.mult))
                wait(dve, tot_done, j.counts(1))
                link(dve.tensor_reduce(pi_sum[:], PI[:].rearrange("p b h -> p h b"), AX_X, ALU.add), follows=False)

            def pi_totals(j):
                if not has(j):
                    return
                link = chain(sm_step, j.counts(SM_STEPS, SM_PI_SUM))
                wait(dve, tot_done, j.counts(1, 1))
                link(at_channels(pick[:], tot_ps))
                link(dve.tensor_reduce(pi_tot[:, 0, :], pick[:], AX_X, ALU.add))
                link(dve.tensor_scalar(pi_tot[:, 1, :], pi_tot[:, 0, :], SUM_FLOOR, None, ALU.add))
                link(dve.reciprocal(pi_tot[:, 2, :], pi_tot[:, 1, :]))

            def weigh(j, t):
                if not has(j):
                    return
                link = chain(u_step, U_STEPS * j.counts(T, t))
                wait(dve, pi_spread, j.counts(T, t + 1))
                wait(dve, squared, j.counts(T, t + 1))
                wait(dve, w_kept, j.counts(T, t + 1))
                wait(dve, uh_done, j.counts(T, t + 1 - T))
                wait(dve, ul_done, j.counts(T, t + 1 - T))
                link(dve.tensor_tensor_reduce(U[:, t, :], pi_b[:], WS[:, t, :], 1.0, 0.0, ALU.mult, ALU.add,
                                              dots[:, 0, t:t + 1]))
                link(dve.tensor_scalar(dots[:, 1, t:t + 1], dots[:, 0, t:t + 1], pi_tot[:, 2, t:t + 1], 1.0,
                                       ALU.mult, ALU.add))
                link(dve.reciprocal(dots[:, 2, t:t + 1], dots[:, 1, t:t + 1]))
                link(dve.scalar_tensor_tensor(U[:, t, :], WV[:, t, :], dots[:, 2, t:t + 1], pi_b[:], ALU.mult,
                                              ALU.mult), follows=False)

            def finish(j, t):
                if not has(j):
                    return
                wait(dve, m2_done, j.counts(T, t + 1))
                dve.scalar_tensor_tensor(x_tile(j, t), acc[:, (t + 1) % 2, :], bias[:, t:t + 1], x_tile(j, t),
                                         ALU.add, ALU.add).then_inc(y_done, 1)

            def step(i):
                finish(i - 2, 2)
                weigh(i - 1, 1)
                weigh(i - 1, 2)
                group_stats(i + 1)
                head_sum_weights(i)
                group_norm(i + 1)
                finish(i - 1, 0)
                softmax_shift(i)
                softmax_divide(i)
                finish(i - 1, 1)
                pi_totals(i)
                weigh(i, 0)

            pipeline(dve, step, -1, B + 1)


_INS = ["x", "L0_conv_qkv_w", "L0_conv_temp", "L0_conv_out_w", "L0_conv_out_b"]


def kernel(**inputs):
    import numpy as _np
    import concourse.bacc as _bacc
    from concourse import mybir as _mybir
    from concourse.bass_utils import run_bass_kernel_spmd as _run

    nc = _bacc.Bacc("TRN2", target_bir_lowering=False, num_devices=1)
    arrays, args = {}, []
    for name in _INS:
        a = _np.ascontiguousarray(inputs[name])
        arrays[f"in_{name}"] = a
        args.append(nc.dram_tensor(f"in_{name}", a.shape, _mybir.dt.from_np(a.dtype), kind="ExternalInput").ap())
    shape = arrays["in_x"].shape
    args.append(nc.dram_tensor("out_y", shape, _mybir.dt.float32, kind="ExternalOutput").ap())
    conv_attention(nc, *args)
    r = _run(nc, [arrays], core_ids=[0])
    return r.results[0]["out_y"]
```

```python
from contextlib import ExitStack

import concourse.bass as bass
from concourse import mybir

ALU = mybir.AluOpType
ACT = mybir.ActivationFunctionType
F32 = mybir.dt.float32
F32R = mybir.dt.float32r
I32 = mybir.dt.int32
AX_X = mybir.AxisListType.X

P = 128
GROUPS = 32
GN_EPS = 1e-5
NORM_FLOOR = 1e-12
SUM_FLOOR = 1e-8
SLOTS = 4
BANK = 512
QUAD = 32
RSQRT_SEED = 0x5F3759DF
NEWTON = 3

GN_MEASURED, GN_AGGREGATED, GN_SPREAD, GN_STEPS = 1, 2, 5, 9 + 3 * NEWTON
HEADSUM_STEPS = 4
SM_SHIFTED, SM_PI, SM_PI_SUM, SM_STEPS = 3, 6, 7, 11
U_STEPS = 4


class Image:

    def __init__(self, number, slot):
        self.number, self.slot = number, slot % SLOTS

    def __add__(self, n):
        return Image(self.number + n, self.slot + n)

    def __sub__(self, n):
        return self + -n

    def follows(self, n):
        return not isinstance(self.number, int) or self.number >= n

    def counts(self, each, more=0):
        return self.number * each + more

    def of(self, dram):
        known = isinstance(self.number, int)
        return dram[self.number] if known else dram[bass.ds(self.number, 1)].squeeze(0)


FIRST = Image(0, 0)


def conv_attention(nc, x, qkv_w, temp, out_w, out_b, y):
    B, C, H, W = x.shape
    N = H * W
    HEADS = temp.shape[0]
    D = C // HEADS
    T = C // P
    HPT = P // D
    HALVES = N // BANK
    BLOCKS = N // P
    QUADS = P // QUAD
    PER_GROUP = C // GROUPS // T
    assert D == QUAD and T * P == C and HALVES * BANK == N and PER_GROUP * GROUPS == P

    x_img = x.rearrange("b (p t) h w -> b p (t h w)", t=T)
    y_img = y.rearrange("b (p t) h w -> b p (t h w)", t=T)

    with ExitStack() as ctx:
        def sb(name, shape, dt=F32):
            return ctx.enter_context(nc.sbuf_tensor(name, shape, dt))

        def pb(name, shape):
            return ctx.enter_context(nc.psum_tensor(name, shape, F32))

        def sem(name):
            return ctx.enter_context(nc.semaphore(name))

        X = sb("X", [P, SLOTS, T * N])
        XN = sb("XN", [P, T, N])
        XH = sb("XH", [P, T, N], F32R)
        XL = sb("XL", [P, T, N], F32R)
        WV = sb("WV", [P, 2, T, N])
        WS = sb("WS", [P, 2, T, N])
        UH = sb("UH", [P, T, N], F32R)
        UL = sb("UL", [P, T, N], F32R)
        W1H = sb("W1H", [P, T, C], F32R)
        W1L = sb("W1L", [P, T, C], F32R)
        W2H = sb("W2H", [P, T, C], F32R)
        W2L = sb("W2L", [P, T, C], F32R)
        identity = sb("identity", [P, P])
        group_mean = sb("group_mean", [P, P])
        head_mask = sb("head_mask", [P, T, QUAD])
        ones = sb("ones", [P, P])
        temp_row = sb("temp_row", [1, HEADS])
        temp_o = sb("temp_o", [P, T])
        bias = sb("bias", [P, T])
        stats = sb("stats", [P, T * HALVES, 6])
        part_mv = sb("part_mv", [P, 2])
        wait_cell = sb("wait_cell", [P, 1])
        gmean = sb("gmean", [P, 1])
        dmean = sb("dmean", [P, 1])
        spread = sb("spread", [P, 1])
        gvar = sb("gvar", [P, 1])
        seed = sb("seed", [P, 1])
        root = sb("root", [P, 1])
        root_t = sb("root_t", [P, 2])
        rstd = sb("rstd", [P, 2])
        shift = sb("shift", [P, 2])
        sumsq = sb("sumsq", [P, T])
        inv = sb("inv", [P, 3, T])
        headsum = sb("headsum", [P, T, QUAD])
        ST = sb("ST", [P, BLOCKS, QUAD])
        smax = sb("smax", [P, BLOCKS])
        SE = sb("SE", [P, BLOCKS, HEADS])
        EX = sb("EX", [P, BLOCKS, HEADS])
        ssum = sb("ssum", [P, BLOCKS])
        srec = sb("srec", [P, BLOCKS])
        PI = sb("PI", [P, HEADS, BLOCKS])
        pi_sum = sb("pi_sum", [P, HEADS])
        PIT = sb("PIT", [HEADS * BLOCKS, P])
        PIB = sb("PIB", [P, T, N])
        pick = sb("pick", [P, T, HEADS])
        pi_tot = sb("pi_tot", [P, 3, T])
        dots = sb("dots", [P, 3, T])

        pi_dram = nc.dram_tensor("pi", [HEADS, N], F32).ap()

        acc = pb("acc", [P, T, N])
        scores = pb("scores", [P, BANK])
        turned_pi = scores[0:HEADS * BLOCKS, N // QUADS:N // QUADS + P]
        small = pb("small", [P, BANK])
        gn_ps = small[:, 0:2]
        tot_ps = small[:, 16:16 + HEADS]
        temp_ps = scores[:, 0:HEADS]

        first_loaded = [sem(f"first_loaded_{t}") for t in range(T)]
        x_loaded = sem("x_loaded")
        y_stored = sem("y_stored")
        w1_loaded = sem("w1_loaded")
        w2_loaded = sem("w2_loaded")
        consts_loaded = sem("consts_loaded")
        masks_step = sem("masks_step")
        ones_set = sem("ones_set")
        temp_spread = sem("temp_spread")
        temp_kept = sem("temp_kept")
        weights_turned = sem("weights_turned")
        weights_hi = sem("weights_hi")
        weights_lo = sem("weights_lo")
        gn_step = sem("gn_step")
        gmean_done = sem("gmean_done")
        gvar_done = sem("gvar_done")
        xn_done = sem("xn_done")
        xh_done = sem("xh_done")
        xl_done = sem("xl_done")
        m1_done = sem("m1_done")
        squared = sem("squared")
        w_kept = sem("w_kept")
        headsum_step = sem("headsum_step")
        scores_done = sem("scores_done")
        sm_step = sem("sm_step")
        exp_done = sem("exp_done")
        pi_turned = sem("pi_turned")
        pi_kept = sem("pi_kept")
        pi_written = sem("pi_written")
        tot_done = sem("tot_done")
        pi_spread = [sem(f"pi_spread_{t}") for t in range(T)]
        u_step = sem("u_step")
        uh_done = sem("uh_done")
        ul_done = sem("ul_done")
        m2_done = sem("m2_done")
        y_done = sem("y_done")

        def turned(k):
            return acc[:, k // 2, (k % 2) * BANK:(k % 2) * BANK + C]

        raw_w1 = WV[:, 0].rearrange("p t n -> p (t n)")[:, 0:T * C].rearrange("p (t c) -> p t c", t=T)
        raw_w2 = WS[:, 0].rearrange("p t n -> p (t n)")[:, 0:T * C]

        def has(j):
            return not isinstance(j.number, int) or 0 <= j.number < B

        def norm_of(j):
            n = j.slot % 2
            return rstd[:, n:n + 1], shift[:, n:n + 1]

        def w_tile(j, t):
            return WV[:, j.slot % 2, t, :]

        def square_tile(j, t):
            return WS[:, j.slot % 2, t, :]

        def x_tile(j, t):
            return X[:, j.slot, t * N:(t + 1) * N]

        def pipeline(eng, step, first, last):
            loop_first, loop_end = 2, B - 2
            assert (loop_end - loop_first) % SLOTS == 0
            for i in range(first, loop_first):
                step(Image(i, i))
            with eng.Fori(loop_first, loop_end - SLOTS + 1, SLOTS) as i:
                for k in range(SLOTS):
                    step(Image(i + k, loop_first + k))
            for i in range(loop_end, last + 1):
                step(Image(i, i))

        block = ctx.enter_context(nc.Block())

        @block.sync
        def _(sp):
            def load(j):
                if has(j):
                    if j.follows(2):
                        sp.wait_ge(x_loaded, j.counts(16, -16))
                    sp.dma_start(X[:, j.slot, :], j.of(x_img)).then_inc(x_loaded, 16)

            for t in range(T):
                sp.dma_start(x_tile(FIRST, t), FIRST.of(x_img)[:, t * N:(t + 1) * N]).then_inc(first_loaded[t], 16)
            sp.dma_start(raw_w1, qkv_w.rearrange("(t p) c -> p t c", t=T)).then_inc(w1_loaded, 16)
            sp.dma_start(raw_w2, out_w.rearrange("(p t) o -> p (t o)", t=T)).then_inc(w2_loaded, 16)
            for j in range(1, SLOTS):
                load(Image(j, j))

            def store(j, t):
                if has(j):
                    sp.wait_ge(y_done, j.counts(T, t + 1))
                    sp.dma_start(j.of(y_img)[:, t * N:(t + 1) * N], x_tile(j, t)).then_inc(y_stored, 16)

            def spread_pi(j):
                if has(j):
                    sp.wait_ge(pi_kept, j.counts(1, 1))
                    sp.dma_start(pi_dram.rearrange("h (b n) -> (h b) n", n=P), PIT[:]).then_inc(pi_written, 16)
                    sp.wait_ge(pi_written, j.counts(16, 16))
                    for t in range(T):
                        sp.dma_start(PIB[:, t, :], pi_dram[t * HPT:(t + 1) * HPT].unsqueeze(1).to_broadcast([HPT, D, N]))\
                            .then_inc(pi_spread[t], 16)

            def step(i):
                store(i - 2, 2)
                if has(i - 2) and has(i + 2):
                    sp.wait_ge(y_stored, (i - 2).counts(T * 16, T * 16))
                    load(i + 2)
                spread_pi(i)
                store(i - 1, 0)
                store(i - 1, 1)

            pipeline(sp, step, 0, B + 1)
            sp.wait_ge(y_stored, B * T * 16)

        @block.gpsimd
        def _(pool):
            pool.memset(identity[:], 0.0).then_inc(masks_step, 1)
            pool.memset(group_mean[:], 1.0 / PER_GROUP).then_inc(masks_step, 1)
            pool.memset(head_mask[:], 1.0).then_inc(masks_step, 1)
            pool.wait_ge(masks_step, 3)
            groups = group_mean[:].rearrange("p (g k) -> p g k", k=PER_GROUP)
            pool.affine_select(out=identity[:], in_=identity[:], compare_op=ALU.not_equal, fill=1.0, base=0,
                               pattern=[[-1, P]], channel_multiplier=1).then_inc(masks_step, 1)
            pool.affine_select(out=groups, in_=groups, compare_op=ALU.is_ge, fill=0.0, base=0,
                               pattern=[[-PER_GROUP, GROUPS], [0, PER_GROUP]],
                               channel_multiplier=1).then_inc(masks_step, 1)
            pool.affine_select(out=head_mask[:], in_=head_mask[:], compare_op=ALU.is_ge, fill=0.0, base=0,
                               pattern=[[P, T], [-D, QUAD]], channel_multiplier=1).then_inc(masks_step, 1)
            pool.wait_ge(masks_step, 6)
            pool.affine_select(out=groups, in_=groups, compare_op=ALU.is_ge, fill=0.0, base=PER_GROUP - 1,
                               pattern=[[PER_GROUP, GROUPS], [0, PER_GROUP]],
                               channel_multiplier=-1).then_inc(masks_step, 1)
            pool.affine_select(out=head_mask[:], in_=head_mask[:], compare_op=ALU.is_ge, fill=0.0, base=D - 1,
                               pattern=[[-P, T], [D, QUAD]], channel_multiplier=-1).then_inc(masks_step, 1)

            def u_lo(j, t):
                if has(j):
                    pool.wait_ge(uh_done, j.counts(T, t + 1))
                    if j.follows(1):
                        pool.wait_ge(m2_done, j.counts(T))
                    pool.tensor_tensor(UL[:, t, :], w_tile(j, t), UH[:, t, :].bitcast(F32),
                                       ALU.subtract).then_inc(ul_done, 1)

            def x_lo(j, t):
                if has(j) and j.follows(1):
                    pool.wait_ge(xn_done, j.counts(T, t + 1))
                    pool.wait_ge(xh_done, j.counts(T, t + 1))
                    pool.wait_ge(m1_done, j.counts(T))
                    pool.tensor_tensor(XL[:, t, :], XN[:, t, :], XH[:, t, :].bitcast(F32),
                                       ALU.subtract).then_inc(xl_done, 1)

            def step(i):
                for t in range(T):
                    u_lo(i - 1, t)
                for t in range(T):
                    x_lo(i + 1, t)

            pipeline(pool, step, 0, B)

        @block.scalar
        def _(act):
            act.dma_start(temp_row[:], temp.rearrange("h a -> a h")).then_inc(consts_loaded, 16)
            act.dma_start(bias[:], out_b.rearrange("(p t) -> p t", t=T)).then_inc(consts_loaded, 16)
            for k in range(2 * T):
                act.wait_ge(weights_turned, k + 1)
                act.activation(W1H[:, k, :] if k < T else W2H[:, k - T, :], turned(k), ACT.Copy,
                               scale=1.0 if k < T else -1.0).then_inc(weights_hi, 1)

            def step(i):
                def u_hi(t):
                    j = i - 1
                    if has(j):
                        act.wait_ge(u_step, U_STEPS * j.counts(T, t + 1))
                        if j.follows(1):
                            act.wait_ge(m2_done, j.counts(T))
                        if j.follows(1):
                            act.wait_ge(ul_done, j.counts(T, t + 1 - T))
                        act.activation(UH[:, t, :], w_tile(j, t), ACT.Copy).then_inc(uh_done, 1)

                def square_w(t):
                    if has(i):
                        act.wait_ge(m1_done, i.counts(T, t + 1))
                        if i.follows(2):
                            act.wait_ge(u_step, U_STEPS * i.counts(T, t + 1 - 2 * T))
                            act.wait_ge(scores_done, i.counts(1, -1))
                        if i.follows(1):
                            act.wait_ge(headsum_step, i.counts(HEADSUM_STEPS))
                        act.activation(square_tile(i, t), acc[:, t, :], ACT.Square,
                                       accum_out=sumsq[:, t:t + 1]).then_inc(squared, 1)

                def keep_w(t):
                    if has(i):
                        act.wait_ge(m1_done, i.counts(T, t + 1))
                        if i.follows(2):
                            act.wait_ge(uh_done, i.counts(T, t + 1 - 2 * T))
                            act.wait_ge(ul_done, i.counts(T, t + 1 - 2 * T))
                        act.activation(w_tile(i, t), acc[:, t, :], ACT.Copy).then_inc(w_kept, 1)

                def normalise(t):
                    j = i + 1
                    if has(j) and j.follows(1):
                        rstd_j, shift_j = norm_of(j)
                        act.wait_ge(gn_step, j.counts(GN_STEPS, GN_STEPS))
                        act.wait_ge(xl_done, j.counts(T, t + 1 - T))
                        act.activation(XN[:, t, :], x_tile(j, t), ACT.Identity, bias=shift_j,
                                       scale=rstd_j).then_inc(xn_done, 1)

                def x_hi(t):
                    j = i + 1
                    if has(j):
                        rstd_j, shift_j = norm_of(j)
                        act.wait_ge(gn_step, j.counts(GN_STEPS, GN_STEPS))
                        if j.follows(1):
                            act.wait_ge(m1_done, j.counts(T))
                            act.wait_ge(xl_done, j.counts(T, t + 1 - T))
                        act.activation(XH[:, t, :], x_tile(j, t), ACT.Identity, bias=shift_j,
                                       scale=rstd_j).then_inc(xh_done, 1)

                def exponentials():
                    if has(i):
                        act.wait_ge(sm_step, i.counts(SM_STEPS, SM_SHIFTED))
                        act.activation(EX[:], SE[:], ACT.Exp).then_inc(exp_done, 1)

                def keep_pi():
                    if has(i):
                        act.wait_ge(pi_turned, i.counts(1, 1))
                        if i.follows(1):
                            act.wait_ge(pi_written, i.counts(16))
                        act.activation(PIT[:], turned_pi, ACT.Copy).then_inc(pi_kept, 1)

                square_w(0)
                keep_w(0)
                u_hi(0)
                square_w(1)
                u_hi(1)
                keep_w(1)
                u_hi(2)
                square_w(2)
                keep_w(2)
                normalise(0)
                x_hi(0)
                exponentials()
                normalise(1)
                keep_pi()
                x_hi(1)
                normalise(2)
                x_hi(2)

            pipeline(act, step, -1, B)

        @block.tensor
        def _(pe):
            def turn_weights(ks):
                columns1 = raw_w1.rearrange("p o (c k) -> p k o c", k=T)
                columns2 = raw_w2.rearrange("p (m o c) -> p o m c", m=T, o=T)
                for k in ks:
                    for m in range(T):
                        raw = columns1[:, k, m, :] if k < T else columns2[:, k - T, m, :]
                        last = pe.transpose(turned(k)[:, m * P:(m + 1) * P], raw, identity[:])
                    last.then_inc(weights_turned, 1)

            def term(out, m, left, right, n, k):
                w, r = left[n == 1], right[n == 2]
                for h in range(HALVES):
                    last = pe.matmul(out[:, h * BANK:(h + 1) * BANK], w[:, k, m * P:(m + 1) * P],
                                     r[:, k, h * BANK:(h + 1) * BANK], start=(n == 0 and k == 0),
                                     stop=(n == 2 and k == T - 1))
                return last

            def product(out, m, left, right, before, inside):
                order = [(n, k) for k in range(T) for n in (0, 1)] + [(2, k) for k in range(T)]
                for n, k in order:
                    before(n, k)
                    if (n, k) in inside:
                        inside[n, k]()
                    last = term(out, m, left, right, n, k)
                return last

            def first_product(i, t, inside):
                def before(n, k):
                    if t == 0 and n == 0:
                        pe.wait_ge(xh_done, i.counts(T, k + 1))
                    if t == 0 and n == 2:
                        pe.wait_ge(xl_done, i.counts(T, k + 1))

                if has(i):
                    if i.follows(2):
                        pe.wait_ge(y_done, i.counts(T, t + 1 - 2 * T))
                    elif i.follows(1):
                        pe.wait_ge(squared, i.counts(T, t + 1 - T))
                        pe.wait_ge(w_kept, i.counts(T, t + 1 - T))
                    product(acc[:, t, :], t, (W1H, W1L), (XH, XL), before, inside).then_inc(m1_done, 1)

            def second_product(j, t, inside):
                def before(n, k):
                    if t == 0 and n == 0:
                        pe.wait_ge(uh_done, j.counts(T, k + 1))
                    if t == 0 and n == 2:
                        pe.wait_ge(ul_done, j.counts(T, k + 1))

                if not has(j):
                    for other in inside.values():
                        other()
                    return
                pe.wait_ge(squared, (j + 1).counts(T, t + 1))
                pe.wait_ge(w_kept, (j + 1).counts(T, t + 1))
                product(acc[:, t, :], t, (W2H, W2L), (UH, UL), before, inside).then_inc(m2_done, 1)

            def last_product(j):
                for k in range(T):
                    last_k = k == T - 1
                    for n, t in [(n, t) for n in (0, 1) for t in range(T)] + [(2, t) for t in range(T)]:
                        if n == 0 and t == 0:
                            pe.wait_ge(uh_done, j.counts(T, k + 1))
                        if n == 2 and t == 0:
                            pe.wait_ge(ul_done, j.counts(T, k + 1))
                        if n == 0 and k == 0:
                            pe.wait_ge(y_done, j.counts(T, t + 1 - T))
                        last = term(acc[:, t, :], t, (W2H, W2L), (UH, UL), n, k)
                        if n == 2 and last_k:
                            last.then_inc(m2_done, 1)

            def group_means(j):
                if has(j):
                    if has(j - 2):
                        pe.wait_ge(sm_step, (j - 2).counts(SM_STEPS, SM_PI_SUM + 1))
                    pe.wait_ge(gn_step, j.counts(GN_STEPS, GN_AGGREGATED))
                    pe.matmul(gn_ps[:, 0:1], group_mean[:], part_mv[:, 0:1], start=True, stop=True).then_inc(gmean_done, 1)

            def group_variances(j):
                if has(j):
                    pe.wait_ge(gn_step, j.counts(GN_STEPS, GN_SPREAD))
                    pe.matmul(gn_ps[:, 1:2], group_mean[:], spread[:], start=True, stop=True).then_inc(gvar_done, 1)

            def head_sums(i):
                if not has(i):
                    return
                pe.wait_ge(headsum_step, i.counts(HEADSUM_STEPS, HEADSUM_STEPS))
                pe.wait_ge(squared, i.counts(T, T))
                if i.follows(1):
                    pe.wait_ge(sm_step, i.counts(SM_STEPS, 1 - SM_STEPS))
                if i.follows(1):
                    pe.wait_ge(pi_kept, i.counts(1))
                for t in range(T):
                    for q in range(QUADS):
                        block_q = square_tile(i, t).rearrange("p (b q r) -> p q b r", q=QUADS, r=QUAD)[:, q]
                        last = pe.matmul(scores[q * QUAD:(q + 1) * QUAD, 0:N // QUADS], headsum[:, t, :],
                                         block_q, start=(t == 0), stop=(t == T - 1))
                last.then_inc(scores_done, 1)

            def pi_sums(i):
                if has(i):
                    pe.wait_ge(sm_step, i.counts(SM_STEPS, SM_PI_SUM))
                    pe.matmul(tot_ps, ones[:], pi_sum[:], start=True, stop=True).then_inc(tot_done, 1)

            def turn_pi(i):
                if has(i):
                    pe.wait_ge(sm_step, i.counts(SM_STEPS, SM_PI))
                    pe.transpose(turned_pi, PI[:].rearrange("p h b -> p (h b)"), identity[:]).then_inc(pi_turned, 1)

            def step(i):
                if not has(i) and has(i - 1):
                    last_product(i - 1)
                    return
                def means(j):
                    return lambda: group_means(j)

                def variances(j):
                    return lambda: group_variances(j)

                early = {0: ({}, {(0, 0): means(i + 1)}, {(0, 0): variances(i + 1)}),
                         1: ({(2, 0): means(i + 1), (2, 1): variances(i + 1)}, {}, {})}.get(i.number if not i.follows(2) else None, ({}, {}, {}))
                for t in range(T):
                    first_product(i, t, early[t])
                second_product(i - 1, 0, {(2, 0): lambda: head_sums(i)})
                second_product(i - 1, 1, {(1, 1): lambda: turn_pi(i), (2, 0): lambda: pi_sums(i)})
                second_product(i - 1, 2, {(1, 1): means(i + 2), (2, 2): variances(i + 2)} if i.follows(1) else {})

            pe.wait_ge(masks_step, 8)
            group_means(FIRST)
            pe.wait_ge(w1_loaded, 16)
            turn_weights(range(T))
            group_variances(FIRST)
            pe.wait_ge(w2_loaded, 16)
            turn_weights(range(T, 2 * T))
            pe.wait_ge(consts_loaded, 32)
            pe.wait_ge(ones_set, 1)
            pe.matmul(temp_ps, ones[0:1, :], temp_row[0:1, :], start=True, stop=True).then_inc(temp_spread, 1)
            pe.wait_ge(weights_lo, 2 * T)
            pipeline(pe, step, 0, B)

        @block.vector
        def _(dve):
            def at_channels(out, per_head):
                return dve.tensor_tensor(out, head_mask[:, :, 0:HEADS],
                                         per_head.unsqueeze(1).to_broadcast([P, T, HEADS]), ALU.mult)

            dve.memset(ones[:], 1.0).then_inc(ones_set, 1)
            def weights_lower():
                for k in range(2 * T):
                    dve.wait_ge(weights_hi, k + 1)
                    hi, lo = (W1H[:, k, :], W1L[:, k, :]) if k < T else (W2H[:, k - T, :], W2L[:, k - T, :])
                    dve.scalar_tensor_tensor(lo, turned(k), 1.0 if k < T else -1.0, hi.bitcast(F32), ALU.mult,
                                             ALU.subtract).then_inc(weights_lo, 1)
                dve.wait_ge(temp_spread, 1)
                at_channels(pick[:], temp_ps).then_inc(temp_kept, 1)
                dve.wait_ge(temp_kept, 1)
                dve.tensor_reduce(temp_o[:], pick[:], AX_X, ALU.add).then_inc(temp_kept, 1)

            def chain(semaphore, base):
                done = [0]

                def link(instruction, follows=True):
                    done[0] += 1
                    instruction.then_inc(semaphore, 1)
                    if follows:
                        dve.wait_ge(semaphore, base + done[0])
                return link

            def group_stats(j, tiles):
                if not has(j):
                    return
                if j.follows(1):
                    dve.wait_ge(x_loaded, j.counts(16))
                for t in tiles:
                    if not j.follows(1):
                        dve.wait_ge(first_loaded[t], 16)
                    for h in range(HALVES):
                        last = dve.bn_stats(stats[:, t * HALVES + h, :], x_tile(j, t)[:, h * BANK:(h + 1) * BANK])
                    if t == T - 1:
                        last.then_inc(gn_step, 1)

            def group_moments(j):
                if not has(j):
                    return
                dve.wait_ge(gn_step, j.counts(GN_STEPS, GN_MEASURED))
                dve.memset(wait_cell[:], 0.0)
                dve.bn_aggr(part_mv[:], stats[:].rearrange("p k s -> p (k s)")).then_inc(gn_step, 1)

            def group_spread(j):
                if not has(j):
                    return
                link = chain(gn_step, j.counts(GN_STEPS, GN_AGGREGATED))
                dve.wait_ge(gmean_done, j.counts(1, 1))
                link(dve.tensor_copy(gmean[:], gn_ps[:, 0:1]))
                link(dve.tensor_tensor(dmean[:], part_mv[:, 0:1], gmean[:], ALU.subtract))
                link(dve.scalar_tensor_tensor(spread[:], dmean[:], dmean[:, 0:1], part_mv[:, 1:2], ALU.mult, ALU.add),
                     follows=False)

            def group_norm(j):
                if not has(j):
                    return
                link = chain(gn_step, j.counts(GN_STEPS, GN_SPREAD))
                rstd_j, shift_j = norm_of(j)
                dve.wait_ge(gvar_done, j.counts(1, 1))
                link(dve.tensor_scalar(gvar[:], gn_ps[:, 1:2], GN_EPS, None, ALU.add))
                link(dve.tensor_scalar(seed[:].bitcast(I32), gvar[:].bitcast(I32), 1, None, ALU.logical_shift_right))
                link(dve.tensor_scalar(root[:].bitcast(I32), seed[:].bitcast(I32), -1.0, float(RSQRT_SEED),
                                       ALU.mult, ALU.add))
                for n in range(NEWTON):
                    link(dve.scalar_tensor_tensor(root_t[:, 0:1], root[:], root[:, 0:1], gvar[:], ALU.mult, ALU.mult))
                    link(dve.tensor_scalar(root_t[:, 1:2], root_t[:, 0:1], -0.5, 1.5, ALU.mult, ALU.add))
                    if n == NEWTON - 1 and j.follows(2):
                        dve.wait_ge(xn_done, j.counts(T, -T))
                        dve.wait_ge(xh_done, j.counts(T, -T))
                    link(dve.tensor_tensor(rstd_j if n == NEWTON - 1 else root[:], root[:], root_t[:, 1:2], ALU.mult))
                link(dve.scalar_tensor_tensor(shift_j, gmean[:], -1.0, rstd_j, ALU.mult, ALU.mult), follows=False)

            def normalise_first():
                rstd_j, shift_j = norm_of(FIRST)
                dve.wait_ge(gn_step, GN_STEPS)
                for t in range(T):
                    dve.tensor_scalar(XN[:, t, :], x_tile(FIRST, t), rstd_j, shift_j, ALU.mult, ALU.add)\
                        .then_inc(xn_done, 1)
                    dve.wait_ge(xn_done, t + 1)
                    dve.wait_ge(xh_done, t + 1)
                    dve.tensor_tensor(XL[:, t, :], XN[:, t, :], XH[:, t, :].bitcast(F32), ALU.subtract)\
                        .then_inc(xl_done, 1)

            def head_sum_weights(j):
                if not has(j):
                    return
                link = chain(headsum_step, j.counts(HEADSUM_STEPS))
                dve.wait_ge(squared, j.counts(T, T))
                link(dve.tensor_scalar(inv[:, 0, :], sumsq[:], NORM_FLOOR ** 2, None, ALU.max))
                link(dve.reciprocal(inv[:, 1, :], inv[:, 0, :]))
                if not j.follows(1):
                    dve.wait_ge(temp_kept, 2)
                link(dve.tensor_tensor(inv[:, 2, :], inv[:, 1, :], temp_o[:], ALU.mult))
                if j.follows(1):
                    dve.wait_ge(scores_done, j.counts(1))
                link(dve.tensor_tensor(headsum[:], head_mask[:],
                                       inv[:, 2, :].unsqueeze(2).to_broadcast([P, T, QUAD]), ALU.mult), follows=False)

            def softmax_shift(j):
                if not has(j):
                    return
                link = chain(sm_step, j.counts(SM_STEPS))
                dve.wait_ge(scores_done, j.counts(1, 1))
                link(dve.transpose(ST[:].rearrange("p b h -> p (b h)"), scores[:, 0:N // QUADS]))
                link(dve.tensor_reduce(smax[:], ST[:, :, 0:HEADS], AX_X, ALU.max))
                link(dve.tensor_tensor(SE[:], ST[:, :, 0:HEADS],
                                       smax[:].unsqueeze(2).to_broadcast([P, BLOCKS, HEADS]), ALU.subtract),
                     follows=False)

            def softmax_divide(j):
                if not has(j):
                    return
                link = chain(sm_step, j.counts(SM_STEPS, SM_SHIFTED))
                dve.wait_ge(exp_done, j.counts(1, 1))
                link(dve.tensor_reduce(ssum[:], EX[:], AX_X, ALU.add))
                link(dve.reciprocal(srec[:], ssum[:]))
                if j.follows(1):
                    dve.wait_ge(pi_turned, j.counts(1))
                link(dve.tensor_tensor(PI[:].rearrange("p h b -> p b h"), EX[:], srec[:].unsqueeze(2).to_broadcast([P, BLOCKS, HEADS]), ALU.mult))
                if j.follows(1):
                    dve.wait_ge(tot_done, j.counts(1))
                link(dve.tensor_reduce(pi_sum[:], PI[:], AX_X, ALU.add), follows=False)

            def pi_totals(j):
                if not has(j):
                    return
                link = chain(sm_step, j.counts(SM_STEPS, SM_PI_SUM))
                dve.wait_ge(tot_done, j.counts(1, 1))
                link(at_channels(pick[:], tot_ps))
                link(dve.tensor_reduce(pi_tot[:, 0, :], pick[:], AX_X, ALU.add))
                link(dve.tensor_scalar(pi_tot[:, 1, :], pi_tot[:, 0, :], SUM_FLOOR, None, ALU.add))
                link(dve.reciprocal(pi_tot[:, 2, :], pi_tot[:, 1, :]))

            def weigh(j, t):
                if not has(j):
                    return
                link = chain(u_step, U_STEPS * j.counts(T, t))
                dve.wait_ge(pi_spread[t], j.counts(16, 16))
                dve.wait_ge(squared, j.counts(T, t + 1))
                dve.wait_ge(w_kept, j.counts(T, t + 1))
                dve.wait_ge(scores_done, j.counts(1, 1))
                link(dve.tensor_tensor_reduce(square_tile(j, t), PIB[:, t, :], square_tile(j, t), 1.0, 0.0, ALU.mult, ALU.add,
                                              dots[:, 0, t:t + 1]))
                link(dve.tensor_scalar(dots[:, 1, t:t + 1], dots[:, 0, t:t + 1], pi_tot[:, 2, t:t + 1], 1.0,
                                       ALU.mult, ALU.add))
                link(dve.reciprocal(dots[:, 2, t:t + 1], dots[:, 1, t:t + 1]))
                link(dve.scalar_tensor_tensor(w_tile(j, t), w_tile(j, t), dots[:, 2, t:t + 1], PIB[:, t, :], ALU.mult,
                                              ALU.mult), follows=False)

            def finish(j, t):
                if not has(j):
                    return
                dve.wait_ge(m2_done, j.counts(T, t + 1))
                dve.scalar_tensor_tensor(x_tile(j, t), acc[:, t, :], bias[:, t:t + 1], x_tile(j, t),
                                         ALU.add, ALU.add).then_inc(y_done, 1)

            def step(i):
                weigh(i - 1, 0)
                finish(i - 2, 2)
                weigh(i - 1, 1)
                weigh(i - 1, 2)
                if i.follows(0):
                    group_norm(i + 1)
                head_sum_weights(i)
                group_stats(i + 2, [0])
                softmax_shift(i)
                softmax_divide(i)
                group_stats(i + 2, range(1, T))
                group_moments(i + 2)
                finish(i - 1, 0)
                pi_totals(i)
                finish(i - 1, 1)
                group_spread(i + 2)

            group_stats(FIRST, range(T))
            group_moments(FIRST)
            group_spread(FIRST)
            group_norm(FIRST)
            weights_lower()
            normalise_first()
            pipeline(dve, step, -1, B + 1)


_INS = ["x", "L0_conv_qkv_w", "L0_conv_temp", "L0_conv_out_w", "L0_conv_out_b"]


def kernel(**inputs):
    import numpy as _np
    import concourse.bacc as _bacc
    from concourse import mybir as _mybir
    from concourse.bass_utils import run_bass_kernel_spmd as _run

    nc = _bacc.Bacc("TRN2", target_bir_lowering=False, num_devices=1)
    arrays, args = {}, []
    for name in _INS:
        a = _np.ascontiguousarray(inputs[name])
        arrays[f"in_{name}"] = a
        args.append(nc.dram_tensor(f"in_{name}", a.shape, _mybir.dt.from_np(a.dtype), kind="ExternalInput").ap())
    shape = arrays["in_x"].shape
    args.append(nc.dram_tensor("out_y", shape, _mybir.dt.float32, kind="ExternalOutput").ap())
    conv_attention(nc, *args)
    r = _run(nc, [arrays], core_ids=[0])
    return r.results[0]["out_y"]
```

```python
from contextlib import ExitStack

import concourse.bass as bass
from concourse import mybir

ALU = mybir.AluOpType
ACT = mybir.ActivationFunctionType
F32 = mybir.dt.float32
F32R = mybir.dt.float32r
I32 = mybir.dt.int32
AX_X = mybir.AxisListType.X

P = 128
GROUPS = 32
GN_EPS = 1e-5
NORM_FLOOR = 1e-12
SUM_FLOOR = 1e-8
SLOTS = 4
BANK = 512
QUAD = 32
RSQRT_SEED = 0x5F3759DF
NEWTON = 3

NEWTON_STEPS = 3
GN_MEASURED, GN_AGGREGATED, GN_SEEDED = 1, 2, 11
GN_ROOTED = GN_SEEDED + NEWTON * NEWTON_STEPS
GN_STEPS = GN_ROOTED + 3
HEADSUM_STEPS = 3
SM_SHIFTED, SM_STEPS = 3, 6
U_STEPS = 6


class Image:

    def __init__(self, number, slot):
        self.number, self.slot = number, slot % SLOTS

    def __add__(self, n):
        return Image(self.number + n, self.slot + n)

    def __sub__(self, n):
        return self + -n

    def follows(self, n):
        return not isinstance(self.number, int) or self.number >= n

    def counts(self, each, more=0):
        return self.number * each + more

    def of(self, dram):
        known = isinstance(self.number, int)
        return dram[self.number] if known else dram[bass.ds(self.number, 1)].squeeze(0)


FIRST = Image(0, 0)


def conv_attention(nc, x, qkv_w, temp, out_w, out_b, y):
    B, C, H, W = x.shape
    N = H * W
    HEADS = temp.shape[0]
    D = C // HEADS
    T = C // P
    HPT = P // D
    HALVES = N // BANK
    BLOCKS = N // P
    QUADS = P // QUAD
    PER_GROUP = C // GROUPS // T
    assert NEWTON == T and D == QUAD and T * P == C and HALVES * BANK == N and PER_GROUP * GROUPS == P

    x_img = x.rearrange("b (p t) h w -> b p (t h w)", t=T)
    y_img = y.rearrange("b (p t) h w -> b p (t h w)", t=T)

    with ExitStack() as ctx:
        def sb(name, shape, dt=F32):
            return ctx.enter_context(nc.sbuf_tensor(name, shape, dt))

        def pb(name, shape):
            return ctx.enter_context(nc.psum_tensor(name, shape, F32))

        def sem(name):
            return ctx.enter_context(nc.semaphore(name))

        X = sb("X", [P, SLOTS, T * N])
        XN = sb("XN", [P, T, N])
        XH = sb("XH", [P, T, N], F32R)
        XL = sb("XL", [P, T, N], F32R)
        WV = sb("WV", [P, 2, T, N])
        WS = sb("WS", [P, 2, T, N])
        UH = sb("UH", [P, T, N], F32R)
        UL = sb("UL", [P, T, N], F32R)
        W1H = sb("W1H", [P, T, C], F32R)
        W1L = sb("W1L", [P, T, C], F32R)
        W2H = sb("W2H", [P, T, C], F32R)
        W2L = sb("W2L", [P, T, C], F32R)
        identity = sb("identity", [P, P])
        head_mask = sb("head_mask", [P, T, QUAD])
        ones = sb("ones", [P, P])
        temp_row = sb("temp_row", [1, HEADS])
        temp_o = sb("temp_o", [P, T])
        head_temp = sb("head_temp", [P, T, QUAD])
        bias = sb("bias", [P, T])
        stats = sb("stats", [P, T * HALVES, 6])
        wait_cell = sb("wait_cell", [P, 1])
        part_mv = sb("part_mv", [P, 2, QUAD])
        turned_mv = sb("turned_mv", [P, 2, QUAD])
        gsum = sb("gsum", [P, QUAD // PER_GROUP])
        dmean = sb("dmean", [P, QUAD])
        dmean2 = sb("dmean2", [P, QUAD])
        spread = sb("spread", [P, QUAD])
        gvarsum = sb("gvarsum", [P, QUAD // PER_GROUP])
        gvar = sb("gvar", [P, QUAD // PER_GROUP])
        seed = sb("seed", [P, QUAD // PER_GROUP])
        root = sb("root", [P, QUAD // PER_GROUP])
        root_t = sb("root_t", [P, 2, QUAD // PER_GROUP])
        turned_norm = sb("turned_norm", [P, 2, QUAD])
        norm = sb("norm", [P, 2, 2, QUAD])
        sumsq = sb("sumsq", [P, T])
        inv = sb("inv", [P, 2, T])
        headsum = sb("headsum", [P, T, QUAD])
        ST = sb("ST", [P, BLOCKS, QUAD])
        smax = sb("smax", [P, BLOCKS])
        SE = sb("SE", [P, BLOCKS, HEADS])
        EX = sb("EX", [P, BLOCKS, HEADS])
        ssum = sb("ssum", [P, BLOCKS])
        srec = sb("srec", [P, BLOCKS])
        PI = sb("PI", [P, HEADS, BLOCKS])
        PIT = sb("PIT", [HEADS * BLOCKS, P + 1])
        PIB = sb("PIB", [P, T, BLOCKS, P + 1])
        pick = sb("pick", [P, T, HEADS])
        pi_tot = sb("pi_tot", [P, T])
        dots = sb("dots", [P, 4, T])

        pi_dram = nc.dram_tensor("pi", [HEADS, BLOCKS * (P + 1)], F32).ap()

        acc = pb("acc", [P, T, N])
        scores = pb("scores", [P, BANK])
        turned_pi = scores[0:HEADS * BLOCKS, N // QUADS:N // QUADS + P]
        small = pb("small", [P, BANK])
        temp_ps = scores[:, C:C + HEADS]

        first_loaded = [sem(f"first_loaded_{t}") for t in range(T)]
        x_loaded = sem("x_loaded")
        y_stored = sem("y_stored")
        w1_loaded = sem("w1_loaded")
        w2_loaded = sem("w2_loaded")
        consts_loaded = sem("consts_loaded")
        masks_step = sem("masks_step")
        ones_set = sem("ones_set")
        temp_spread = sem("temp_spread")
        temp_kept = sem("temp_kept")
        weights_turned = sem("weights_turned")
        weights_hi = sem("weights_hi")
        weights_lo = sem("weights_lo")
        gn_step = sem("gn_step")
        xn_done = sem("xn_done")
        xh_done = sem("xh_done")
        xl_done = sem("xl_done")
        m1_done = sem("m1_done")
        squared = sem("squared")
        w_kept = sem("w_kept")
        headsum_step = sem("headsum_step")
        scores_done = sem("scores_done")
        sm_step = sem("sm_step")
        exp_done = sem("exp_done")
        pi_turned = sem("pi_turned")
        pi_kept = sem("pi_kept")
        pi_written = sem("pi_written")
        pi_spread = [sem(f"pi_spread_{t}") for t in range(T)]
        u_step = sem("u_step")
        uh_done = sem("uh_done")
        ul_done = [sem(f"ul_done_{t}") for t in range(T)]
        m2_done = sem("m2_done")
        y_done = sem("y_done")
        biased = sem("biased")
        last_y_done = sem("last_y_done")

        def turned(k):
            if k in (T, T + 1):
                return (scores, small)[k - T][:, 0:C]
            bank = k if k < T else T * HALVES - 1
            return acc[:, bank // HALVES, (bank % HALVES) * BANK:(bank % HALVES) * BANK + C]

        raw_w1 = WV[:, 0].rearrange("p t n -> p (t n)")[:, 0:T * C].rearrange("p (t c) -> p t c", t=T)
        raw_w2 = WS[:, 0].rearrange("p t n -> p (t n)")[:, 0:T * C]

        def has(j):
            return not isinstance(j.number, int) or 0 <= j.number < B

        def norm_of(j):
            return norm[:, j.slot % 2, 0, 0:1], norm[:, j.slot % 2, 1, 0:1]

        def w_tile(j, t):
            return WV[:, j.slot % 2, t, :]

        def square_tile(j, t):
            return WS[:, j.slot % 2, t, :]

        def x_tile(j, t):
            return X[:, j.slot, t * N:(t + 1) * N]

        def pipeline(eng, step, first, last):
            loop_first, loop_end = 2, B - 2
            assert (loop_end - loop_first) % SLOTS == 0
            for i in range(first, loop_first):
                step(Image(i, i))
            with eng.Fori(loop_first, loop_end - SLOTS + 1, SLOTS) as i:
                for k in range(SLOTS):
                    step(Image(i + k, loop_first + k))
            for i in range(loop_end, last + 1):
                step(Image(i, i))

        block = ctx.enter_context(nc.Block())

        @block.sync
        def _(sp):
            def load(j):
                if has(j):
                    if j.follows(2):
                        sp.wait_ge(x_loaded, j.counts(16, -16))
                    sp.dma_start(X[:, j.slot, :], j.of(x_img)).then_inc(x_loaded, 16)

            for t in range(T):
                sp.dma_start(x_tile(FIRST, t), FIRST.of(x_img)[:, t * N:(t + 1) * N]).then_inc(first_loaded[t], 16)
            sp.dma_start(raw_w1, qkv_w.rearrange("(t p) c -> p t c", t=T)).then_inc(w1_loaded, 16)
            sp.dma_start(raw_w2, out_w.rearrange("(p t) o -> p (t o)", t=T)).then_inc(w2_loaded, 16)
            for j in range(1, SLOTS):
                load(Image(j, j))

            def store(j, t):
                if has(j):
                    if t < T - 1:
                        sp.wait_ge(y_done, j.counts(T - 1, t + 1))
                    else:
                        sp.wait_ge(last_y_done, j.counts(1, 1))
                    sp.dma_start(j.of(y_img)[:, t * N:(t + 1) * N], x_tile(j, t)).then_inc(y_stored, 16)

            def spread_pi(j):
                if has(j):
                    sp.wait_ge(pi_kept, j.counts(1, 1))
                    sp.dma_start(pi_dram.rearrange("h (b n) -> (h b) n", n=P + 1), PIT[:]).then_inc(pi_written, 16)
                    sp.wait_ge(pi_written, j.counts(16, 16))
                    for t in range(T):
                        heads = pi_dram[t * HPT:(t + 1) * HPT].unsqueeze(1).to_broadcast([HPT, D, BLOCKS * (P + 1)])
                        sp.dma_start(PIB[:, t].rearrange("p b n -> p (b n)"), heads).then_inc(pi_spread[t], 16)

            def step(i):
                store(i - 2, 2)
                if has(i - 2) and has(i + 2):
                    sp.wait_ge(y_stored, (i - 2).counts(T * 16, T * 16))
                    load(i + 2)
                spread_pi(i)
                store(i - 1, 0)
                store(i - 1, 1)

            pipeline(sp, step, 0, B + 1)
            sp.wait_ge(y_stored, B * T * 16)

        @block.gpsimd
        def _(pool):
            pool.memset(identity[:], 0.0).then_inc(masks_step, 1)
            pool.memset(head_mask[:], 1.0).then_inc(masks_step, 1)
            pool.wait_ge(masks_step, 2)
            pool.affine_select(out=identity[:], in_=identity[:], compare_op=ALU.not_equal, fill=1.0, base=0,
                               pattern=[[-1, P]], channel_multiplier=1).then_inc(masks_step, 1)
            pool.affine_select(out=head_mask[:], in_=head_mask[:], compare_op=ALU.is_ge, fill=0.0, base=0,
                               pattern=[[P, T], [-D, QUAD]], channel_multiplier=1).then_inc(masks_step, 1)
            pool.wait_ge(masks_step, 4)
            pool.affine_select(out=head_mask[:], in_=head_mask[:], compare_op=ALU.is_ge, fill=0.0, base=D - 1,
                               pattern=[[-P, T], [D, QUAD]], channel_multiplier=-1).then_inc(masks_step, 1)

            def u_lo(j, t):
                if has(j):
                    pool.wait_ge(uh_done, j.counts(T, t + 1))
                    if j.follows(1):
                        pool.wait_ge(m2_done, j.counts(T))
                    pool.tensor_tensor(UL[:, t, :], w_tile(j, t), UH[:, t, :].bitcast(F32),
                                       ALU.subtract).then_inc(ul_done[t], 1)

            def add_x(j):
                if has(j) and has(j + 1):
                    pool.wait_ge(biased, j.counts(1, 1))
                    pool.tensor_tensor(x_tile(j, T - 1), square_tile(j, T - 1), x_tile(j, T - 1),
                                       ALU.add).then_inc(last_y_done, 1)

            def x_lo(j, t):
                if has(j) and j.follows(1):
                    pool.wait_ge(xn_done, j.counts(T, t + 1))
                    pool.wait_ge(xh_done, j.counts(T, t + 1))
                    pool.wait_ge(m1_done, j.counts(T))
                    pool.tensor_tensor(XL[:, t, :], XN[:, t, :], XH[:, t, :].bitcast(F32),
                                       ALU.subtract).then_inc(xl_done, 1)

            def step(i):
                add_x(i - 2)
                u_lo(i - 1, 0)
                for t in range(T):
                    x_lo(i + 1, t)

            pipeline(pool, step, 0, B)

        @block.scalar
        def _(act):
            act.dma_start(temp_row[:], temp.rearrange("h a -> a h")).then_inc(consts_loaded, 16)
            act.dma_start(bias[:], out_b.rearrange("(p t) -> p t", t=T)).then_inc(consts_loaded, 16)
            for k in range(2 * T):
                act.wait_ge(weights_turned, k + 1)
                act.activation(W1H[:, k, :] if k < T else W2H[:, k - T, :], turned(k), ACT.Copy,
                               scale=1.0 if k < T else -1.0).then_inc(weights_hi, 1)

            def step(i):
                def u_hi(t):
                    j = i - 1
                    if has(j):
                        act.wait_ge(u_step, U_STEPS * j.counts(T, t + 1))
                        if j.follows(1):
                            act.wait_ge(m2_done, j.counts(T))
                            act.wait_ge(ul_done[t], j.counts(1))
                        act.activation(UH[:, t, :], w_tile(j, t), ACT.Copy).then_inc(uh_done, 1)

                def square_w(t):
                    if has(i):
                        act.wait_ge(m1_done, i.counts(T, t + 1))
                        if i.follows(2):
                            act.wait_ge(u_step, U_STEPS * i.counts(T, t + 1 - 2 * T))
                            act.wait_ge(scores_done, i.counts(1, -1))
                            if t == T - 1:
                                act.wait_ge(last_y_done, i.counts(1, -1))
                        if i.follows(1):
                            act.wait_ge(headsum_step, i.counts(HEADSUM_STEPS))
                        act.activation(square_tile(i, t), acc[:, t, :], ACT.Square,
                                       accum_out=sumsq[:, t:t + 1]).then_inc(squared, 1)

                def keep_w(t):
                    if has(i):
                        act.wait_ge(m1_done, i.counts(T, t + 1))
                        if i.follows(2):
                            act.wait_ge(uh_done, i.counts(T, t + 1 - 2 * T))
                            act.wait_ge(ul_done[t], i.counts(1, -1))
                        act.activation(w_tile(i, t), acc[:, t, :], ACT.Copy).then_inc(w_kept, 1)

                def add_bias(j):
                    if has(j) and has(j + 1):
                        act.wait_ge(m2_done, j.counts(T, T))
                        act.activation(square_tile(j, T - 1), acc[:, T - 1, :], ACT.Identity,
                                       bias=bias[:, T - 1:T]).then_inc(biased, 1)

                def normalise(t):
                    j = i + 1
                    if has(j) and j.follows(1):
                        rstd_j, shift_j = norm_of(j)
                        act.wait_ge(gn_step, j.counts(GN_STEPS, GN_STEPS))
                        act.wait_ge(xl_done, j.counts(T, t + 1 - T))
                        act.activation(XN[:, t, :], x_tile(j, t), ACT.Identity, bias=shift_j,
                                       scale=rstd_j).then_inc(xn_done, 1)

                def x_hi(t):
                    j = i + 1
                    if has(j):
                        rstd_j, shift_j = norm_of(j)
                        act.wait_ge(gn_step, j.counts(GN_STEPS, GN_STEPS))
                        if j.follows(1):
                            act.wait_ge(m1_done, j.counts(T))
                            act.wait_ge(xl_done, j.counts(T, t + 1 - T))
                        act.activation(XH[:, t, :], x_tile(j, t), ACT.Identity, bias=shift_j,
                                       scale=rstd_j).then_inc(xh_done, 1)

                def exponentials():
                    if has(i):
                        act.wait_ge(sm_step, i.counts(SM_STEPS, SM_SHIFTED))
                        act.activation(EX[:], SE[:], ACT.Exp).then_inc(exp_done, 1)

                def keep_pi():
                    if has(i):
                        act.wait_ge(pi_turned, i.counts(1, 1))
                        if i.follows(1):
                            act.wait_ge(pi_written, i.counts(16))
                        act.activation(PIT[:, 0:P], turned_pi, ACT.Copy, accum_out=PIT[:, P:P + 1]).then_inc(pi_kept, 1)

                add_bias(i - 2)
                square_w(0)
                keep_w(0)
                u_hi(0)
                square_w(1)
                u_hi(1)
                keep_w(1)
                u_hi(2)
                square_w(2)
                keep_w(2)
                normalise(0)
                x_hi(0)
                exponentials()
                normalise(1)
                keep_pi()
                x_hi(1)
                normalise(2)
                x_hi(2)

            pipeline(act, step, -1, B)

        @block.tensor
        def _(pe):
            def turn_weights(ks):
                columns1 = raw_w1.rearrange("p o (c k) -> p k o c", k=T)
                columns2 = raw_w2.rearrange("p (m o c) -> p o m c", m=T, o=T)
                for k in ks:
                    for m in range(T):
                        raw = columns1[:, k, m, :] if k < T else columns2[:, k - T, m, :]
                        last = pe.transpose(turned(k)[:, m * P:(m + 1) * P], raw, identity[:])
                    last.then_inc(weights_turned, 1)

            def term(out, m, left, right, n, k):
                w, r = left[n == 1], right[n == 2]
                for h in range(HALVES):
                    last = pe.matmul(out[:, h * BANK:(h + 1) * BANK], w[:, k, m * P:(m + 1) * P],
                                     r[:, k, h * BANK:(h + 1) * BANK], start=(n == 0 and k == 0),
                                     stop=(n == 2 and k == T - 1))
                return last

            def product(out, m, left, right, before, inside):
                order = [(n, k) for k in range(T) for n in (0, 1)] + [(2, k) for k in range(T)]
                for n, k in order:
                    before(n, k)
                    if (n, k) in inside:
                        inside[n, k]()
                    last = term(out, m, left, right, n, k)
                return last

            def acc_left(j, t):
                if t < T - 1:
                    pe.wait_ge(y_done, j.counts(T - 1, t + 1))
                else:
                    pe.wait_ge(biased, j.counts(1, 1))

            def first_product(i, t):
                def before(n, k):
                    if t == 0 and n == 0:
                        pe.wait_ge(xh_done, i.counts(T, k + 1))
                    if t == 0 and n == 2:
                        pe.wait_ge(xl_done, i.counts(T, k + 1))

                if has(i):
                    if not i.follows(1) and t == T - 1:
                        pe.wait_ge(weights_lo, 2 * T)
                    if i.follows(2):
                        acc_left(i - 2, t)
                    elif i.follows(1):
                        pe.wait_ge(squared, i.counts(T, t + 1 - T))
                        pe.wait_ge(w_kept, i.counts(T, t + 1 - T))
                    product(acc[:, t, :], t, (W1H, W1L), (XH, XL), before, {}).then_inc(m1_done, 1)

            def second_product(j, t, inside):
                def before(n, k):
                    if t == 0 and n == 0:
                        pe.wait_ge(uh_done, j.counts(T, k + 1))
                    if t == 0 and n == 2:
                        pe.wait_ge(ul_done[k], j.counts(1, 1))

                if not has(j):
                    for other in inside.values():
                        other()
                    return
                pe.wait_ge(squared, (j + 1).counts(T, t + 1))
                pe.wait_ge(w_kept, (j + 1).counts(T, t + 1))
                product(acc[:, t, :], t, (W2H, W2L), (UH, UL), before, inside).then_inc(m2_done, 1)

            def last_product(j):
                for k in range(T):
                    last_k = k == T - 1
                    for n, t in [(n, t) for n in (0, 1) for t in range(T)] + [(2, t) for t in range(T)]:
                        if n == 0 and t == 0:
                            pe.wait_ge(uh_done, j.counts(T, k + 1))
                        if n == 2 and t == 0:
                            pe.wait_ge(ul_done[k], j.counts(1, 1))
                        if n == 0 and k == 0:
                            acc_left(j - 1, t)
                        last = term(acc[:, t, :], t, (W2H, W2L), (UH, UL), n, k)
                        if n == 2 and last_k:
                            last.then_inc(m2_done, 1)

            def head_sums(i):
                if not has(i):
                    return
                pe.wait_ge(headsum_step, i.counts(HEADSUM_STEPS, HEADSUM_STEPS))
                pe.wait_ge(squared, i.counts(T, T))
                if i.follows(1):
                    pe.wait_ge(sm_step, i.counts(SM_STEPS, 1 - SM_STEPS))
                    pe.wait_ge(pi_kept, i.counts(1))
                for t in range(T):
                    for q in range(QUADS):
                        block_q = square_tile(i, t).rearrange("p (b q r) -> p q b r", q=QUADS, r=QUAD)[:, q]
                        last = pe.matmul(scores[q * QUAD:(q + 1) * QUAD, 0:N // QUADS], headsum[:, t, :],
                                         block_q, start=(t == 0), stop=(t == T - 1))
                last.then_inc(scores_done, 1)

            def turn_pi(i):
                if has(i):
                    pe.wait_ge(sm_step, i.counts(SM_STEPS, SM_STEPS))
                    pe.transpose(turned_pi, PI[:].rearrange("p h b -> p (h b)"), identity[:]).then_inc(pi_turned, 1)

            def step(i):
                if not has(i) and has(i - 1):
                    last_product(i - 1)
                    return
                for t in range(T):
                    first_product(i, t)
                second_product(i - 1, 0, {(2, 0): lambda: head_sums(i)})
                turn_at = (1, 1) if has(i + 1) else (0, 0)
                second_product(i - 1, 1, {turn_at: lambda: turn_pi(i)})
                second_product(i - 1, 2, {})

            pe.wait_ge(consts_loaded, 32)
            pe.wait_ge(ones_set, 1)
            pe.matmul(temp_ps, ones[0:1, :], temp_row[0:1, :], start=True, stop=True).then_inc(temp_spread, 1)
            pe.wait_ge(masks_step, 5)
            pe.wait_ge(w1_loaded, 16)
            turn_weights(range(T))
            pe.wait_ge(w2_loaded, 16)
            pe.wait_ge(temp_kept, 1)
            turn_weights(range(T, 2 * T))
            pe.wait_ge(weights_lo, T)
            pipeline(pe, step, 0, B)

        @block.vector
        def _(dve):
            def at_channels(out, per_head):
                return dve.tensor_tensor(out, head_mask[:, :, 0:HEADS],
                                         per_head.unsqueeze(1).to_broadcast([P, T, HEADS]), ALU.mult)

            dve.memset(ones[:], 1.0).then_inc(ones_set, 1)
            dve.memset(part_mv[:], 0.0).then_inc(ones_set, 1)

            def weights_lower(ks):
                for k in ks:
                    dve.wait_ge(weights_hi, k + 1)
                    hi, lo = (W1H[:, k, :], W1L[:, k, :]) if k < T else (W2H[:, k - T, :], W2L[:, k - T, :])
                    dve.scalar_tensor_tensor(lo, turned(k), 1.0 if k < T else -1.0, hi.bitcast(F32), ALU.mult,
                                             ALU.subtract).then_inc(weights_lo, 1)

            def chain(semaphore, base):
                done = [0]

                def link(instruction, follows=True):
                    done[0] += 1
                    instruction.then_inc(semaphore, 1)
                    if follows:
                        dve.wait_ge(semaphore, base + done[0])
                return link

            def group_stats(j, tiles):
                if not has(j):
                    return
                if j.follows(1):
                    dve.wait_ge(x_loaded, j.counts(16))
                for t in tiles:
                    if not j.follows(1):
                        dve.wait_ge(first_loaded[t], 16)
                    for h in range(HALVES):
                        last = dve.bn_stats(stats[:, t * HALVES + h, :], x_tile(j, t)[:, h * BANK:(h + 1) * BANK])
                    if t == T - 1:
                        last.then_inc(gn_step, 1)

            def group_moments(j):
                if not has(j):
                    return
                dve.wait_ge(gn_step, j.counts(GN_STEPS, GN_MEASURED))
                dve.memset(wait_cell[:], 0.0)
                dve.bn_aggr(part_mv[:, :, 0], stats[:].rearrange("p k s -> p (k s)")).then_inc(gn_step, 1)

            def over_groups(row):
                return row.rearrange("p (g k) -> p g k", k=PER_GROUP)

            def to_partitions(row):
                return row.unsqueeze(2).to_broadcast([P, QUAD // PER_GROUP, PER_GROUP])

            def group_variances(j):
                if not has(j):
                    return
                link = chain(gn_step, j.counts(GN_STEPS, GN_AGGREGATED))
                dve.wait_ge(gn_step, j.counts(GN_STEPS, GN_AGGREGATED))
                link(dve.transpose(turned_mv[:].rearrange("p k q -> p (k q)"),
                                   part_mv[:].rearrange("p k q -> p (k q)")))
                link(dve.tensor_reduce(gsum[:], over_groups(turned_mv[:, 0, :]), AX_X, ALU.add))
                link(dve.scalar_tensor_tensor(over_groups(dmean[:]), to_partitions(gsum[:]), 1.0 / PER_GROUP,
                                              over_groups(turned_mv[:, 0, :]), ALU.mult, ALU.subtract))
                link(dve.tensor_tensor(dmean2[:], dmean[:], dmean[:], ALU.mult))
                link(dve.tensor_tensor(spread[:], dmean2[:], turned_mv[:, 1, :], ALU.add))
                link(dve.tensor_reduce(gvarsum[:], over_groups(spread[:]), AX_X, ALU.add))
                link(dve.tensor_scalar(gvar[:], gvarsum[:], 1.0 / PER_GROUP, GN_EPS, ALU.mult, ALU.add))
                link(dve.tensor_scalar(seed[:].bitcast(I32), gvar[:].bitcast(I32), 1, None, ALU.logical_shift_right))
                link(dve.tensor_scalar(root[:].bitcast(I32), seed[:].bitcast(I32), -1.0, float(RSQRT_SEED),
                                       ALU.mult, ALU.add), follows=False)

            def newton(j, n, step):
                if not has(j):
                    return
                dve.wait_ge(gn_step, j.counts(GN_STEPS, GN_SEEDED + n * NEWTON_STEPS + step))
                if step == 0:
                    done = dve.scalar_tensor_tensor(root_t[:, 0, :], root[:], -0.5, root[:], ALU.mult, ALU.mult)
                elif step == 1:
                    done = dve.tensor_tensor(root_t[:, 1, :], root_t[:, 0, :], gvar[:], ALU.mult)
                else:
                    done = dve.scalar_tensor_tensor(root[:], root_t[:, 1, :], 1.5, root[:], ALU.add, ALU.mult)
                done.then_inc(gn_step, 1)

            def group_norm(j):
                if not has(j):
                    return
                link = chain(gn_step, j.counts(GN_STEPS, GN_ROOTED))
                dve.wait_ge(gn_step, j.counts(GN_STEPS, GN_ROOTED))
                link(dve.tensor_copy(over_groups(turned_norm[:, 0, :]), to_partitions(root[:])))
                link(dve.scalar_tensor_tensor(over_groups(turned_norm[:, 1, :]), to_partitions(gsum[:]),
                                              -1.0 / PER_GROUP, to_partitions(root[:]), ALU.mult, ALU.mult))
                if j.follows(2):
                    dve.wait_ge(xn_done, j.counts(T, -T))
                    dve.wait_ge(xh_done, j.counts(T, -T))
                link(dve.transpose(norm[:, j.slot % 2].rearrange("p k q -> p (k q)"),
                                   turned_norm[:].rearrange("p k q -> p (k q)")), follows=False)

            def normalise_first():
                rstd_j, shift_j = norm_of(FIRST)
                dve.wait_ge(gn_step, GN_STEPS)
                for t in range(T):
                    dve.tensor_scalar(XN[:, t, :], x_tile(FIRST, t), rstd_j, shift_j, ALU.mult, ALU.add)\
                        .then_inc(xn_done, 1)

            def lower_first():
                for t in range(T):
                    dve.wait_ge(xn_done, t + 1)
                    dve.wait_ge(xh_done, t + 1)
                    dve.tensor_tensor(XL[:, t, :], XN[:, t, :], XH[:, t, :].bitcast(F32), ALU.subtract)\
                        .then_inc(xl_done, 1)

            def head_sum_weights(j):
                if not has(j):
                    return
                link = chain(headsum_step, j.counts(HEADSUM_STEPS))
                dve.wait_ge(squared, j.counts(T, T))
                link(dve.tensor_scalar(inv[:, 0, :], sumsq[:], NORM_FLOOR ** 2, None, ALU.max))
                link(dve.reciprocal(inv[:, 1, :], inv[:, 0, :]))
                if j.follows(1):
                    dve.wait_ge(scores_done, j.counts(1))
                else:
                    dve.wait_ge(temp_kept, 3)
                link(dve.tensor_tensor(headsum[:], head_temp[:],
                                       inv[:, 1, :].unsqueeze(2).to_broadcast([P, T, QUAD]), ALU.mult), follows=False)

            def softmax_shift(j):
                if not has(j):
                    return
                link = chain(sm_step, j.counts(SM_STEPS))
                dve.wait_ge(scores_done, j.counts(1, 1))
                link(dve.transpose(ST[:].rearrange("p b h -> p (b h)"), scores[:, 0:N // QUADS]))
                link(dve.tensor_reduce(smax[:], ST[:, :, 0:HEADS], AX_X, ALU.max))
                link(dve.tensor_tensor(SE[:], ST[:, :, 0:HEADS],
                                       smax[:].unsqueeze(2).to_broadcast([P, BLOCKS, HEADS]), ALU.subtract),
                     follows=False)

            def softmax_divide(j):
                if not has(j):
                    return
                link = chain(sm_step, j.counts(SM_STEPS, SM_SHIFTED))
                dve.wait_ge(exp_done, j.counts(1, 1))
                link(dve.tensor_reduce(ssum[:], EX[:], AX_X, ALU.add))
                link(dve.reciprocal(srec[:], ssum[:]))
                if j.follows(1):
                    dve.wait_ge(pi_turned, j.counts(1))
                link(dve.tensor_tensor(PI[:].rearrange("p h b -> p b h"), EX[:],
                                       srec[:].unsqueeze(2).to_broadcast([P, BLOCKS, HEADS]), ALU.mult),
                     follows=False)

            def in_blocks(tile):
                return tile.rearrange("p (b n) -> p b n", n=P)

            def weigh(j, t):
                if has(j):
                    pi = PIB[:, t, :, 0:P]
                    total = pi_tot[:, t:t + 1]
                    dot, both, inverse, part = (dots[:, n, t:t + 1] for n in range(4))
                    base = j.counts(U_STEPS * T, U_STEPS * t)
                    dve.wait_ge(pi_spread[t], j.counts(16, 16))
                    dve.tensor_reduce(total, PIB[:, t, :, P], AX_X, ALU.add).then_inc(u_step, 1)
                    dve.wait_ge(squared, j.counts(T, t + 1))
                    dve.wait_ge(scores_done, j.counts(1, 1))
                    dve.tensor_tensor_reduce(in_blocks(square_tile(j, t)), pi, in_blocks(square_tile(j, t)), 1.0, 0.0,
                                             ALU.mult, ALU.add, dot).then_inc(u_step, 1)
                newton(j + 2, t, 0)
                if has(j):
                    dve.wait_ge(u_step, base + 2)
                    dve.scalar_tensor_tensor(both, total, SUM_FLOOR, dot, ALU.add, ALU.add).then_inc(u_step, 1)
                newton(j + 2, t, 1)
                if has(j):
                    dve.wait_ge(u_step, base + 3)
                    dve.reciprocal(inverse, both).then_inc(u_step, 1)
                newton(j + 2, t, 2)
                if has(j):
                    dve.wait_ge(u_step, base + 4)
                    dve.scalar_tensor_tensor(part, total, SUM_FLOOR, inverse, ALU.add, ALU.mult).then_inc(u_step, 1)
                    dve.wait_ge(u_step, base + 5)
                    dve.wait_ge(w_kept, j.counts(T, t + 1))
                    dve.scalar_tensor_tensor(in_blocks(w_tile(j, t)), in_blocks(w_tile(j, t)), part, pi, ALU.mult,
                                             ALU.mult).then_inc(u_step, 1)

            def u_lo(j, t):
                if has(j):
                    dve.wait_ge(uh_done, j.counts(T, t + 1))
                    dve.wait_ge(u_step, j.counts(U_STEPS * T, U_STEPS * (t + 1)))
                    if j.follows(1):
                        dve.wait_ge(m2_done, j.counts(T))
                    dve.tensor_tensor(UL[:, t, :], w_tile(j, t), UH[:, t, :].bitcast(F32),
                                      ALU.subtract).then_inc(ul_done[t], 1)

            def finish(j, t):
                if not has(j):
                    return
                dve.wait_ge(m2_done, j.counts(T, t + 1))
                if t < T - 1:
                    done = y_done
                else:
                    dve.wait_ge(last_y_done, j.counts(1))
                    done = last_y_done
                dve.scalar_tensor_tensor(x_tile(j, t), acc[:, t, :], bias[:, t:t + 1], x_tile(j, t),
                                         ALU.add, ALU.add).then_inc(done, 1)

            def step(i):
                weigh(i - 1, 0)
                if not has(i - 1):
                    finish(i - 2, 2)
                weigh(i - 1, 1)
                weigh(i - 1, 2)
                group_norm(i + 1)
                u_lo(i - 1, 1)
                head_sum_weights(i)
                u_lo(i - 1, 2)
                group_stats(i + 2, [0])
                softmax_shift(i)
                softmax_divide(i)
                group_stats(i + 2, range(1, T))
                group_moments(i + 2)
                finish(i - 1, 0)
                finish(i - 1, 1)
                group_variances(i + 2)

            group_stats(FIRST, range(T))
            dve.wait_ge(temp_spread, 1)
            dve.wait_ge(masks_step, 5)
            at_channels(pick[:], temp_ps).then_inc(temp_kept, 1)
            dve.wait_ge(temp_kept, 1)
            dve.tensor_reduce(temp_o[:], pick[:], AX_X, ALU.add).then_inc(temp_kept, 1)
            dve.wait_ge(ones_set, 2)
            group_moments(FIRST)
            group_variances(FIRST)
            for n in range(NEWTON):
                for k in range(NEWTON_STEPS):
                    newton(FIRST, n, k)
            group_norm(FIRST)
            weights_lower(range(T))
            normalise_first()
            lower_first()
            weights_lower(range(T, 2 * T))
            dve.wait_ge(temp_kept, 2)
            dve.tensor_tensor(head_temp[:], head_mask[:], temp_o[:].unsqueeze(2).to_broadcast([P, T, QUAD]),
                              ALU.mult).then_inc(temp_kept, 1)
            group_stats(FIRST + 1, range(T))
            group_moments(FIRST + 1)
            group_variances(FIRST + 1)
            pipeline(dve, step, 0, B + 1)


_INS = ["x", "L0_conv_qkv_w", "L0_conv_temp", "L0_conv_out_w", "L0_conv_out_b"]


def kernel(**inputs):
    import numpy as _np
    import concourse.bacc as _bacc
    from concourse import mybir as _mybir
    from concourse.bass_utils import run_bass_kernel_spmd as _run

    nc = _bacc.Bacc("TRN2", target_bir_lowering=False, num_devices=1)
    arrays, args = {}, []
    for name in _INS:
        a = _np.ascontiguousarray(inputs[name])
        arrays[f"in_{name}"] = a
        args.append(nc.dram_tensor(f"in_{name}", a.shape, _mybir.dt.from_np(a.dtype), kind="ExternalInput").ap())
    shape = arrays["in_x"].shape
    args.append(nc.dram_tensor("out_y", shape, _mybir.dt.float32, kind="ExternalOutput").ap())
    conv_attention(nc, *args)
    r = _run(nc, [arrays], core_ids=[0])
    return r.results[0]["out_y"]
```
